# Optimizing a Trainium2 kernel written in Bass

```python
import numpy as np
import jax
import jax.numpy as jnp

def _softmax(x, axis=-1):
    return jax.nn.softmax(x, axis=axis)

def _gelu(x):
    return jax.nn.gelu(x, approximate=True)

def _silu(x):
    return jax.nn.silu(x)

def _sigmoid(x):
    return jax.nn.sigmoid(x)

def _layernorm(x, axis=-1, eps=1e-05):
    m = jnp.mean(x, axis=axis, keepdims=True)
    v = jnp.var(x, axis=axis, keepdims=True)
    return (x - m) / jnp.sqrt(v + eps)

def _scatter_add(tgt, idx, src, axis=0):
    return tgt.at[idx].add(src)

def _segment_sum(src, seg, n):
    return jax.ops.segment_sum(src, seg, n)
kernel_name = 'mk_macaron_d1_jaxref_r8_1ba0fc'

def setup_inputs(seed: int=0):
    np.random.seed(seed)
    _w = jnp.asarray

    def _L0_attn_setup():
        import jax, jax.numpy as jnp
        import numpy as np
        DIM = 128
        HEADS = 16
        DIM_HEAD = 64
        INNER = HEADS * DIM_HEAD
        EPS = 1e-10

        def safe_softmax(s):
            m = jnp.max(s, axis=-1, keepdims=True)
            e = jnp.exp(s - m)
            return e / (jnp.sum(e, axis=-1, keepdims=True) + EPS)
        key = jax.random.key(seed)
        ks = jax.random.split(key, 6)
        B, N = (4, 256)
        x = jax.random.normal(ks[0], (B, N, DIM), dtype=jnp.float32)
        s_in = 1.0 / np.sqrt(DIM)
        s_inner = 1.0 / np.sqrt(INNER)
        Wq = jax.random.uniform(ks[1], (INNER, DIM), jnp.float32, -s_in, s_in)
        Wk = jax.random.uniform(ks[2], (INNER, DIM), jnp.float32, -s_in, s_in)
        Wv = jax.random.uniform(ks[3], (INNER, DIM), jnp.float32, -s_in, s_in)
        Wo = jax.random.uniform(ks[4], (DIM, INNER), jnp.float32, -s_inner, s_inner)
        bo = jax.random.uniform(ks[5], (DIM,), jnp.float32, -s_inner, s_inner)
        return {'x': x, 'Wq': Wq, 'Wk': Wk, 'Wv': Wv, 'Wo': Wo, 'bo': bo}
    _L0_attn_in = _L0_attn_setup()

    def _L0_ffn_setup():
        import jax, jax.numpy as jnp
        import numpy as np
        TOP_K = 8
        key = jax.random.key(seed)
        k0, k1, k2, k3, k4 = jax.random.split(key, 5)
        B, S, D, E, F = (4, 256, 128, 64, 96)
        scale = 0.02
        return {'hidden_states': jax.random.normal(k0, (B, S, D), dtype=jnp.float32), 'gate_w': jax.random.normal(k1, (E, D), dtype=jnp.float32) * scale, 'gate_proj': jax.random.normal(k2, (E, D, F), dtype=jnp.float32) * scale, 'up_proj': jax.random.normal(k3, (E, D, F), dtype=jnp.float32) * scale, 'down_proj': jax.random.normal(k4, (E, F, D), dtype=jnp.float32) * scale}
    _L0_ffn_in = _L0_ffn_setup()
    _d = {'L0_attn_x': _L0_attn_in['x'], 'L0_attn_Wq': _L0_attn_in['Wq'], 'L0_attn_Wk': _L0_attn_in['Wk'], 'L0_attn_Wv': _L0_attn_in['Wv'], 'L0_attn_Wo': _L0_attn_in['Wo'], 'L0_attn_bo': _L0_attn_in['bo'], 'L0_ffn_gate_w': _L0_ffn_in['gate_w'], 'L0_ffn_gate_proj': _L0_ffn_in['gate_proj'], 'L0_ffn_up_proj': _L0_ffn_in['up_proj'], 'L0_ffn_down_proj': _L0_ffn_in['down_proj']}
    _x0 = _d['L0_attn_x']
    _d['L0_attn_x'] = jax.random.normal(jax.random.fold_in(jax.random.key(seed), 1), (16, 256, 128), dtype=_x0.dtype)
    del _x0
    return _d

def reference(L0_attn_x, L0_attn_Wq, L0_attn_Wk, L0_attn_Wv, L0_attn_Wo, L0_attn_bo, L0_ffn_gate_w, L0_ffn_gate_proj, L0_ffn_up_proj, L0_ffn_down_proj):

    def _L0_attn_ref(x, Wq, Wk, Wv, Wo, bo):
        import jax, jax.numpy as jnp
        import numpy as np
        DIM = 128
        HEADS = 16
        DIM_HEAD = 64
        INNER = HEADS * DIM_HEAD
        EPS = 1e-10

        def safe_softmax(s):
            m = jnp.max(s, axis=-1, keepdims=True)
            e = jnp.exp(s - m)
            return e / (jnp.sum(e, axis=-1, keepdims=True) + EPS)
        B, N, _ = x.shape
        scale = DIM_HEAD ** (-0.5)

        def split_heads(t):
            return t.reshape(B, N, HEADS, DIM_HEAD).transpose(0, 2, 1, 3)
        q = split_heads(x @ Wq.T)
        k = split_heads(x @ Wk.T)
        v = split_heads(x @ Wv.T)
        sim = jnp.einsum('bhid,bhjd->bhij', q, k) * scale
        attn = safe_softmax(sim)
        out = jnp.einsum('bhij,bhjd->bhid', attn, v)
        out = out.transpose(0, 2, 1, 3).reshape(B, N, INNER)
        return out @ Wo.T + bo

    def _L0_ffn_ref(hidden_states, gate_w, gate_proj, up_proj, down_proj):
        import jax, jax.numpy as jnp
        import numpy as np
        TOP_K = 8
        B, S, D = hidden_states.shape
        E = gate_w.shape[0]
        x = hidden_states.reshape(-1, D)
        T = x.shape[0]
        logits = x @ gate_w.T
        probs = jax.nn.softmax(logits, axis=-1)
        top_w, top_i = jax.lax.top_k(probs, TOP_K)
        top_w = top_w / jnp.sum(top_w, axis=-1, keepdims=True)
        cw = jnp.zeros((T, E), dtype=x.dtype).at[jnp.arange(T)[:, None], top_i].add(top_w)

        def step(acc, params):
            wg, wu, wd, w_e = params
            h = jax.nn.silu(x @ wg) * (x @ wu)
            return (acc + h @ wd * w_e[:, None], None)
        acc0 = jnp.zeros_like(x)
        out, _ = jax.lax.scan(step, acc0, (gate_proj, up_proj, down_proj, cw.T))
        return out.reshape(B, S, D)
    x = L0_attn_x
    x = x + 0.5 * _L0_ffn_ref(_layernorm(x, axis=-1), L0_ffn_gate_w, L0_ffn_gate_proj, L0_ffn_up_proj, L0_ffn_down_proj)
    x = x + _L0_attn_ref(_layernorm(x, axis=-1), L0_attn_Wq, L0_attn_Wk, L0_attn_Wv, L0_attn_Wo, L0_attn_bo)
    x = x + 0.5 * _L0_ffn_ref(_layernorm(x, axis=-1), L0_ffn_gate_w, L0_ffn_gate_proj, L0_ffn_up_proj, L0_ffn_down_proj)
    return x

_drawn_inputs = setup_inputs


def setup_inputs(seed=0):
    import zlib

    import numpy as np

    out = dict(_drawn_inputs(seed))
    spreads = {}
    factors = {'L0_attn_Wq': 4.633,
     'L0_attn_Wk': 4.598,
     'L0_attn_bo': 2.804,
     'L0_ffn_gate_w': 8.0,
     'L0_ffn_gate_proj': 8.0,
     'L0_ffn_up_proj': 8.0,
     'L0_ffn_down_proj': 8.0}
    for name, (base, spread) in spreads.items():
        noise = np.random.default_rng([zlib.crc32(name.encode()), seed]).standard_normal(out[name].shape)
        drawn = base * np.exp(spread * noise) if base else spread * noise
        out[name] = jnp.asarray(drawn.astype(out[name].dtype))
    for name, factor in factors.items():
        out[name] = (out[name] * factor).astype(out[name].dtype)
    return out
```

```python
import concourse.bass as bass
from concourse import mybir
from contextlib import ExitStack

FP32 = mybir.dt.float32
FP32R = mybir.dt.float32r
ALU = mybir.AluOpType
ACT = mybir.ActivationFunctionType
AX = mybir.AxisListType

P = 128
D = 128
BATCH, SEQ = 16, 256
E, F, TOP_K = 64, 96, 8
HEADS, DH = 16, 64
INNER = HEADS * DH
LN_EPS, SOFTMAX_EPS = 1e-5, 1e-10

TILES = BATCH * SEQ // P
BT = 4
NB = BT * P
BLOCKS = TILES // BT
GE = 4
GROUPS = E // GE
FS = P // GE
CPG = F // FS
CHUNKS = GROUPS * CPG
GW = CPG * P
UNROLL = 2
LAG = 2
PAIR_CHUNKS = UNROLL * CHUNKS

STATS_AT, NORM_AT, TURN_AT, SPLIT_AT, LOGIT_AT, SHIFT_AT = 3, 6, 9, 11, 14, 17
EXP_AT, PROB_AT, TOP_AT, PICK_AT, WEIGHT_AT, WTURN_AT, WCOPY_AT = 19, 22, 25, 28, 31, 34, 36

PAIRS = HEADS // 2


def macaron_block(nc, x, wq, wk, wv, wo, bo, gate_w, gate_proj, up_proj, down_proj, out):
    x_v = x.rearrange("b (p s) d -> p b (s d)", s=2)
    out_v = out.rearrange("b (p s) d -> p b (s d)", s=2)

    ctx = ExitStack()
    with ctx:
        def sb(name, shape, dt=FP32, scope=ctx):
            return scope.enter_context(nc.sbuf_tensor(name, shape, dt))

        def sem(name):
            return ctx.enter_context(nc.semaphore(name))

        gate_hi = sb("gate_hi", [P, GROUPS, GW], FP32R)
        gate_lo = sb("gate_lo", [P, GROUPS, GW], FP32R)
        up_hi = sb("up_hi", [P, GROUPS, GW], FP32R)
        up_lo = sb("up_lo", [P, GROUPS, GW], FP32R)
        xs = sb("xs", [P, TILES + BT, D])
        spread = sb("spread", [P, GROUPS, P], FP32R)
        ident = sb("ident", [P, P])
        rw = sb("rw", [P, E])
        rw_hi = sb("rw_hi", [P, E], FP32R)
        rw_lo = sb("rw_lo", [P, E], FP32R)
        bias_o = sb("bias_o", [P, 1])
        stats = sb("stats", [P, BT, 6])
        mean_var = sb("mean_var", [P, BT, 2])
        var_eps = sb("var_eps", [P, BT])
        rstd = sb("rstd", [P, BT])
        neg_half = sb("neg_half", [P, BT])
        spare = sb("spare", [P, 1])

        with ExitStack() as ffn_scope:
            def fb(name, shape, dt=FP32):
                return sb(name, shape, dt, ffn_scope)
            down_hi = fb("down_hi", [P, GROUPS, GW], FP32R)
            down_lo = fb("down_lo", [P, GROUPS, GW], FP32R)
            act_buf = fb("act_buf", [P, 3, NB])
            h_hi = fb("h_hi", [P, 2, NB], FP32R)
            h_lo = fb("h_lo", [P, 2, NB], FP32R)
            xnT_hi = fb("xnT_hi", [P, 2, NB], FP32R)
            xnT_lo = fb("xnT_lo", [P, 2, NB], FP32R)
            wT = fb("wT", [P, 2, NB], FP32R)
            rows = fb("rows", [P, BT, D])
            yT = fb("yT", [P, NB])
            probs = fb("probs", [P, BT, E])
            rest = fb("rest", [P, BT, E])
            best = fb("best", [P, BT, TOP_K])
            col = fb("col", [P, 6, BT])

        with ExitStack() as attn_scope:
            def ab(name, shape, dt=FP32):
                return sb(name, shape, dt, attn_scope)
            wq_s = ab("wq_s", [P, INNER])
            wk_s = ab("wk_s", [P, INNER])
            wv_s = ab("wv_s", [P, INNER])
            wo_s = ab("wo_s", [P, PAIRS, D])
            qT = ab("qT", [P, PAIRS, SEQ])
            kT = ab("kT", [P, PAIRS, SEQ])
            v_s = ab("v_s", [P, 2, INNER])
            prob = ab("prob", [P, 3, 2, SEQ])
            probT = ab("probT", [P, 4, 2, SEQ])
            ctxT = ab("ctxT", [P, PAIRS, SEQ])
            a_rows = ab("a_rows", [P, 2, D])
            a_xnT = ab("a_xnT", [P, SEQ])
            a_yT = ab("a_yT", [P, SEQ])
            neg_max = ab("neg_max", [P, HEADS, 2])
            row_sum = ab("row_sum", [P, HEADS, 2])
            row_inv = ab("row_inv", [P, HEADS, 2])

        bank = [ctx.enter_context(nc.psum_tensor(f"bank{i}", [P, 512], FP32)) for i in range(8)]

        consts = sem("consts")
        x_in = sem("x_in")
        x_out = sem("x_out")
        small_in = sem("small_in")
        rw_split = sem("rw_split")

        def feed_forward(block, ph, loads):
            def s(name):
                return sem(f"{name}{ph}")
            stage_in = [s(f"stage_in{k}_") for k in range(3)]
            stage_hi, stage_lo = s("stage_hi"), s("stage_lo")
            chain = s("chain")
            var_ready, rstd_ready, xn_ready = s("var_ready"), s("rstd_ready"), s("xn_ready")
            xn_turned, xnT_ready = s("xn_turned"), s("xnT_ready")
            logits_done, shifted, exp_done = s("logits_done"), s("shifted"), s("exp_done")
            weights_ready, weights_turned, wT_ready = s("weights_ready"), s("weights_turned"), s("wT_ready")
            spread_done, gate_done, up_done = s("spread_done"), s("gate_done"), s("up_done")
            silu_done, scaled, h_done = s("silu_done"), s("scaled"), s("h_done")
            hi_done, lo_done, down_done = s("hi_done"), s("lo_done"), s("down_done")
            yT_done, y_turned, x_added = s("yT_done"), s("y_turned"), s("x_added")

            gate_ps, up_ps, w_ps = bank[0:2], bank[2:4], bank[4:6]
            y_ps, aux = bank[6], bank[7]
            LOADS = [(v[:, g, :], hi[:, g, :], lo[:, g, :]) for g in range(GROUPS) for v, hi, lo in loads]

            def positions():
                for c in range(PAIR_CHUNKS + LAG):
                    yield c, c // CHUNKS, c % CHUNKS

            @block.sync
            def _(sp):
                if ph == 0:
                    sp.dma_start(xs[:, 0:BT, :].rearrange("p (b s) d -> p b (s d)", s=2), x_v[:, 0:2, :]).then_inc(x_in, 16)
                for n, (view, _hi, _lo) in enumerate(LOADS):
                    if n >= 3:
                        sp.wait_ge(stage_lo, n - 2)
                    sp.dma_start(act_buf[:, n % 3, 0:GW], view).then_inc(stage_in[n % 3], 16)
                if ph == 1:
                    with sp.Fori(0, BLOCKS) as i:
                        sp.wait_ge(x_added, i + 1)
                        sp.dma_start(out_v[:, bass.ds(2 * i, 2), :],
                                     xs[:, bass.ds(BT * i, BT), :].rearrange("p (b s) d -> p b (s d)", s=2)).then_inc(x_out, 16)
                    sp.wait_ge(x_out, 16 * BLOCKS)

            @block.gpsimd
            def _(pool):
                if ph == 0:
                    nc.gpsimd.memset(ident[:, :], 0.0).then_inc(consts, 1)
                    nc.gpsimd.memset(spread[:, :, :].bitcast(FP32), 0.0).then_inc(consts, 1)
                    nc.gpsimd.memset(neg_half[:, :], -0.5).then_inc(consts, 1)
                    nc.gpsimd.memset(xs[:, TILES:TILES + BT, :], 0.0).then_inc(consts, 1)
                    pool.wait_ge(consts, 4)
                    nc.gpsimd.affine_select(out=ident[:, :], in_=ident[:, :], compare_op=ALU.not_equal, fill=1.0,
                                            base=0, pattern=[[-1, P]], channel_multiplier=1).then_inc(consts, 1)
                    wide = spread[:, :, :].rearrange("p g (i k) -> p (g i) k", k=FS)
                    nc.gpsimd.affine_select(out=wide, in_=wide.bitcast(FP32), compare_op=ALU.not_equal, fill=1.0,
                                            base=0, pattern=[[-1, E], [0, FS]], channel_multiplier=1).then_inc(consts, 1)
                    pool.wait_ge(consts, 6)
                    nc.gpsimd.affine_select(out=wide, in_=wide.bitcast(FP32), compare_op=ALU.not_equal, fill=1.0,
                                            base=-E, pattern=[[-1, E], [0, FS]], channel_multiplier=1).then_inc(consts, 1)

                def rstd_of(count):
                    pool.wait_ge(var_ready, count)
                    nc.gpsimd.tensor_tensor(rstd[:, :], var_eps[:, :], neg_half[:, :], ALU.pow).then_inc(rstd_ready, 1)

                rstd_of(1)
                with pool.Fori(0, BLOCKS // UNROLL) as i:
                    for c, blk, k in positions():
                        if c < PAIR_CHUNKS and k == STATS_AT:
                            rstd_of(i * UNROLL + blk + 2)
                        if c < PAIR_CHUNKS:
                            pool.wait_ge(hi_done, i * PAIR_CHUNKS + c + 1)
                            if c >= 2:
                                pool.wait_ge(down_done, i * PAIR_CHUNKS + c - 1)
                            nc.gpsimd.tensor_tensor(h_lo[:, c % 2, :], act_buf[:, c % 3, :], h_hi[:, c % 2, :].bitcast(FP32),
                                                    ALU.subtract).then_inc(lo_done, 1)

            @block.scalar
            def _(act):
                if ph == 0:
                    act.dma_start(rw[:, :], gate_w).then_inc(small_in, 16)
                    act.dma_start(bias_o[:, :], bo).then_inc(small_in, 16)
                    act.dma_start(xs[:, BT:TILES, :].rearrange("p (b s) d -> p b (s d)", s=2), x_v[:, 2:BATCH, :]).then_inc(x_in, 16)

                for n, (_view, hi, _lo) in enumerate(LOADS):
                    act.wait_ge(stage_in[n % 3], 16 * (n // 3 + 1))
                    nc.scalar.activation(hi, act_buf[:, n % 3, 0:GW], ACT.Copy).then_inc(stage_hi, 1)

                def exp_of(count):
                    act.wait_ge(shifted, count)
                    nc.scalar.activation(probs[:, :, :], rest[:, :, :], ACT.Exp).then_inc(exp_done, 1)

                def take_yT(down):
                    act.wait_ge(down_done, down)
                    nc.scalar.activation(yT[:, :], y_ps[:, :], ACT.Copy).then_inc(yT_done, 1)

                exp_of(1)
                with act.Fori(0, BLOCKS // UNROLL) as i:
                    for c, blk, k in positions():
                        if c < PAIR_CHUNKS:
                            act.wait_ge(gate_done, i * PAIR_CHUNKS + c + 1)
                            if c >= 3:
                                act.wait_ge(lo_done, i * PAIR_CHUNKS + c - 2)
                            nc.scalar.activation(act_buf[:, c % 3, :], gate_ps[c % 2][:, :], ACT.Silu).then_inc(silu_done, 1)
                        if 1 <= c <= PAIR_CHUNKS:
                            act.wait_ge(h_done, i * PAIR_CHUNKS + c)
                            if c >= 3:
                                act.wait_ge(down_done, i * PAIR_CHUNKS + c - 2)
                            nc.scalar.activation(h_hi[:, (c - 1) % 2, :], act_buf[:, (c - 1) % 3, :], ACT.Copy).then_inc(hi_done, 1)
                        if c == CHUNKS + LAG:
                            take_yT(i * PAIR_CHUNKS + CHUNKS)
                        if c < PAIR_CHUNKS and k == EXP_AT:
                            exp_of(i * UNROLL + blk + 2)
                    take_yT(i * PAIR_CHUNKS + PAIR_CHUNKS)

            @block.tensor
            def _(pe):
                def split_product(ps, hi, lo, m_hi, m_lo, start, stop):
                    nc.tensor.matmul(ps, hi, m_hi, start=start, stop=False)
                    nc.tensor.matmul(ps, hi, m_lo, start=False, stop=False)
                    return nc.tensor.matmul(ps, lo, m_hi, start=False, stop=stop)

                def turn_rows(ready, count, done):
                    pe.wait_ge(ready, count)
                    for t in range(BT):
                        last = nc.tensor.transpose(aux[:, t * P:(t + 1) * P], rows[:, t, :], ident[:, :])
                    last.then_inc(done, 1)

                def logits(count, slot):
                    pe.wait_ge(xnT_ready, count)
                    for t in range(BT):
                        a, b = t * P, (t + 1) * P
                        last = split_product(aux[:, t * E:(t + 1) * E], xnT_hi[:, slot, a:b], xnT_lo[:, slot, a:b],
                                             rw_hi[:, :], rw_lo[:, :], True, True)
                    last.then_inc(logits_done, 1)

                def turn_y(count, routings):
                    pe.wait_ge(yT_done, count)
                    pe.wait_ge(wT_ready, routings)
                    for t in range(BT):
                        last = nc.tensor.transpose(aux[:, t * P:(t + 1) * P], yT[:, t * P:(t + 1) * P], ident[:, :])
                    last.then_inc(y_turned, 1)

                pe.wait_ge(consts, 7)
                pe.wait_ge(rw_split, 2)
                turn_rows(xn_ready, 1, xn_turned)
                logits(1, 0)
                turn_rows(weights_ready, 2, weights_turned)
                pe.wait_ge(stage_lo, len(LOADS))
                with pe.Fori(0, BLOCKS // UNROLL) as i:
                    for c, blk, k in positions():
                        if c < PAIR_CHUNKS:
                            G, j = k // CPG, k % CPG
                            n = c // CPG
                            if j == 0:
                                if k == 0:
                                    pe.wait_ge(wT_ready, i * UNROLL + blk + 1)
                                if n >= 2:
                                    pe.wait_ge(scaled, i * PAIR_CHUNKS + CPG * (n - 1))
                                nc.tensor.matmul(w_ps[n % 2][:, :], spread[:, G, :], wT[:, blk, :],
                                                 start=True, stop=True).then_inc(spread_done, 1)
                            a, b = j * P, (j + 1) * P
                            if c >= 2:
                                pe.wait_ge(silu_done, i * PAIR_CHUNKS + c - 1)
                            split_product(gate_ps[c % 2][:, :], gate_hi[:, G, a:b], gate_lo[:, G, a:b],
                                          xnT_hi[:, blk, :], xnT_lo[:, blk, :], True, True).then_inc(gate_done, 1)
                            if c >= 2:
                                pe.wait_ge(h_done, i * PAIR_CHUNKS + c - 1)
                            split_product(up_ps[c % 2][:, :], up_hi[:, G, a:b], up_lo[:, G, a:b],
                                          xnT_hi[:, blk, :], xnT_lo[:, blk, :], True, True).then_inc(up_done, 1)
                        if c >= LAG:
                            d = c - LAG
                            kd = d % CHUNKS
                            G, a, b = kd // CPG, (kd % CPG) * P, (kd % CPG + 1) * P
                            pe.wait_ge(lo_done, i * PAIR_CHUNKS + d + 1)
                            if kd == 0 and d > 0:
                                pe.wait_ge(yT_done, i * UNROLL + 1)
                            split_product(y_ps[:, :], down_hi[:, G, a:b], down_lo[:, G, a:b],
                                          h_hi[:, d % 2, :], h_lo[:, d % 2, :], kd == 0, kd == CHUNKS - 1).then_inc(down_done, 1)
                        if c == CHUNKS + LAG:
                            turn_y(i * UNROLL + 1, i * UNROLL + 2)
                        if c < PAIR_CHUNKS:
                            nxt = i * UNROLL + blk + 2
                            if k == TURN_AT:
                                turn_rows(xn_ready, nxt, xn_turned)
                            if k == LOGIT_AT:
                                logits(nxt, 1 - blk)
                            if k == WTURN_AT:
                                turn_rows(weights_ready, 2 * nxt, weights_turned)
                    turn_y(i * UNROLL + 2, i * UNROLL + 3)

            @block.vector
            def _(dve):
                if ph == 0:
                    dve.wait_ge(small_in, 32)
                    nc.vector.tensor_copy(rw_hi[:, :], rw[:, :]).then_inc(rw_split, 1)
                    dve.wait_ge(rw_split, 1)
                    nc.vector.tensor_tensor(rw_lo[:, :], rw[:, :], rw_hi[:, :].bitcast(FP32), ALU.subtract).then_inc(rw_split, 1)
                    dve.wait_ge(x_in, 32)
                    dve.wait_ge(consts, 7)

                CHAIN = 2 + 5 + 7
                def over_experts(a):
                    return a.unsqueeze(2).broadcast_to([P, BT, E])

                def stage(k, tile0, done, nth, slot):
                    def step(ins, n):
                        ins.then_inc(chain, 1)
                        dve.wait_ge(chain, done + n)
                    if k == STATS_AT:
                        for t in range(BT):
                            last = nc.vector.bn_stats(stats[:, t, :], xs[:, bass.ds(tile0 + t, 1), :].rearrange("p a d -> p (a d)"))
                        step(last, 1)
                        nc.vector.memset(spare[:, :], 0.0)
                        for t in range(BT):
                            last = nc.vector.bn_aggr(mean_var[:, t, :], stats[:, t, :])
                        step(last, 2)
                        nc.vector.tensor_scalar(var_eps[:, :], mean_var[:, :, 1], LN_EPS, None, ALU.add).then_inc(var_ready, 1)
                    if k == NORM_AT:
                        dve.wait_ge(rstd_ready, nth)
                        for t in range(BT):
                            last = nc.vector.tensor_scalar(rows[:, t, :], xs[:, bass.ds(tile0 + t, 1), :].rearrange("p a d -> p (a d)"),
                                                           mean_var[:, t, 0:1], rstd[:, t:t + 1], ALU.subtract, ALU.mult)
                        last.then_inc(xn_ready, 1)
                    if k == SPLIT_AT:
                        dve.wait_ge(xn_turned, nth)
                        step(nc.vector.tensor_copy(xnT_hi[:, slot, :], aux[:, :]), 3)
                        nc.vector.tensor_tensor(xnT_lo[:, slot, :], aux[:, :], xnT_hi[:, slot, :].bitcast(FP32),
                                                ALU.subtract).then_inc(xnT_ready, 1)
                    lg = aux[:, 0:BT * E].rearrange("p (t e) -> p t e", e=E)
                    if k == SHIFT_AT:
                        dve.wait_ge(logits_done, nth)
                        step(nc.vector.tensor_reduce(col[:, 0, :], lg, AX.X, ALU.max), 4)
                        nc.vector.tensor_tensor(rest[:, :, :], lg, over_experts(col[:, 0, :]), ALU.subtract).then_inc(shifted, 1)
                    if k == PROB_AT:
                        dve.wait_ge(exp_done, nth)
                        step(nc.vector.tensor_reduce(col[:, 1, :], probs[:, :, :], AX.X, ALU.add), 5)
                        step(nc.vector.reciprocal(col[:, 2, :], col[:, 1, :]), 6)
                        nc.vector.tensor_tensor(probs[:, :, :], probs[:, :, :], over_experts(col[:, 2, :]), ALU.mult).then_inc(chain, 1)
                    if k == TOP_AT:
                        dve.wait_ge(chain, done + 7)
                        nc.vector.memset(spare[:, :], 0.0)
                        for t in range(BT):
                            last = nc.vector.max(best[:, t, :], probs[:, t, :])
                        last.then_inc(chain, 1)
                    if k == PICK_AT:
                        dve.wait_ge(chain, done + 8)
                        nc.vector.memset(spare[:, :], 0.0)
                        for t in range(BT):
                            last = nc.vector.match_replace(rest[:, t, :], best[:, t, :], probs[:, t, :], -1.0)
                        step(last, 9)
                        step(nc.vector.tensor_reduce(col[:, 3, :], best[:, :, :], AX.X, ALU.add), 10)
                        step(nc.vector.reciprocal(col[:, 4, :], col[:, 3, :]), 11)
                    if k == WEIGHT_AT:
                        step(nc.vector.tensor_scalar(col[:, 5, :], col[:, 4, :], -0.5, None, ALU.mult), 12)
                        step(nc.vector.scalar_tensor_tensor(out=rest[:, :, :], in0=rest[:, :, :], scalar=0.0, in1=probs[:, :, :],
                                                            op0=ALU.max, op1=ALU.subtract), 13)
                        nc.vector.tensor_tensor(probs[:, :, :], rest[:, :, :], over_experts(col[:, 5, :]), ALU.mult).then_inc(chain, 1)
                        dve.wait_ge(chain, done + CHAIN)
                        hi = rows[:, :, 0:E].bitcast(FP32R)
                        nc.vector.tensor_copy(hi, probs[:, :, :]).then_inc(weights_ready, 1)
                        dve.wait_ge(weights_ready, 2 * nth - 1)
                        nc.vector.tensor_tensor(rows[:, :, E:2 * E].bitcast(FP32R), probs[:, :, :], rows[:, :, 0:E],
                                                ALU.subtract).then_inc(weights_ready, 1)
                    if k == WCOPY_AT:
                        dve.wait_ge(weights_turned, nth)
                        nc.vector.tensor_copy(wT[:, slot, :], aux[:, :]).then_inc(wT_ready, 1)

                STAGES = (STATS_AT, NORM_AT, SPLIT_AT, SHIFT_AT, PROB_AT, TOP_AT, PICK_AT, WEIGHT_AT, WCOPY_AT)

                def add_y(count, tile0):
                    dve.wait_ge(y_turned, count)
                    here = xs[:, bass.ds(tile0, BT), :]
                    nc.vector.tensor_tensor(here, here, aux[:, :].rearrange("p (t d) -> p t d", d=D), ALU.add).then_inc(x_added, 1)

                def low_part(n):
                    _view, hi, lo = LOADS[n]
                    dve.wait_ge(stage_hi, n + 1)
                    nc.vector.tensor_tensor(lo, act_buf[:, n % 3, 0:GW], hi.bitcast(FP32), ALU.subtract).then_inc(stage_lo, 1)

                for n in range(len(LOADS)):
                    low_part(n)
                for k in STAGES:
                    stage(k, 0, 0, 1, 0)
                with dve.Fori(0, BLOCKS // UNROLL) as i:
                    for c, blk, k in positions():
                        if c < PAIR_CHUNKS:
                            at = i * PAIR_CHUNKS + c + 1
                            G = c // CPG
                            buf = act_buf[:, c % 3, :]
                            dve.wait_ge(silu_done, at)
                            if c % CPG == 0:
                                dve.wait_ge(spread_done, i * (PAIR_CHUNKS // CPG) + G + 1)
                            nc.vector.tensor_tensor(buf, buf, w_ps[G % 2][:, :], ALU.mult).then_inc(scaled, 1)
                            dve.wait_ge(scaled, at)
                            dve.wait_ge(up_done, at)
                            nc.vector.tensor_tensor(buf, buf, up_ps[c % 2][:, :], ALU.mult).then_inc(h_done, 1)
                            if k in STAGES:
                                nth = i * UNROLL + blk + 2
                                stage(k, (i * UNROLL + blk + 1) * BT, (i * UNROLL + blk + 1) * CHAIN, nth, 1 - blk)
                        if c == CHUNKS + LAG:
                            add_y(i * UNROLL + 1, i * UNROLL * BT)
                    add_y(i * UNROLL + 2, (i * UNROLL + 1) * BT)


        def attention(block):
            weights_in = sem("attn_weights_in")
            chain, var_ready, rstd_ready, xn_ready = sem("a_chain"), sem("a_var_ready"), sem("a_rstd_ready"), sem("a_xn_ready")
            xn_turned, xnT_ready, qkv_done = sem("a_xn_turned"), sem("a_xnT_ready"), sem("a_qkv_done")
            even_taken, odd_taken = sem("even_taken"), sem("odd_taken")
            scores_done, max_done, exp_done, inv_ready, scaled = (sem("scores_done"), sem("max_done"), sem("a_exp_done"),
                                                                  sem("inv_ready"), sem("a_scaled"))
            prob_turned, probT_ready, context_done, ctxT_ready = (sem("prob_turned"), sem("probT_ready"),
                                                                  sem("context_done"), sem("ctxT_ready"))
            out_done, outT_ready, out_turned, added = sem("out_done"), sem("outT_ready"), sem("out_turned"), sem("a_added")

            turn_ps = bank[4:6]
            ctx_ps, aux = bank[6], bank[7]
            UNITS = [(w, n) for n in range(PAIRS // 2) for w in "qk"] + [("v", n) for n in range(4)]
            HALF = len(UNITS) // 2
            def score_ps(h):
                return bank[h % 4]

            @block.sync
            def _(sp):
                for a, b in ((wq_s[:, :], wq), (wk_s[:, :], wk), (wv_s[:, :], wv), (wo_s[:, :, :], wo)):
                    sp.dma_start(a, b).then_inc(weights_in, 16)

            @block.gpsimd
            def _(pool):
                with pool.Fori(0, BATCH) as b:
                    pool.wait_ge(var_ready, b + 1)
                    nc.gpsimd.tensor_tensor(rstd[:, 0:2], var_eps[:, 0:2], neg_half[:, 0:2], ALU.pow).then_inc(rstd_ready, 1)

            @block.tensor
            def _(pe):
                pe.wait_ge(weights_in, 64)
                with pe.Fori(0, BATCH) as b:
                    pe.wait_ge(xn_ready, b + 1)
                    for s in range(2):
                        last = nc.tensor.transpose(aux[:, s * P:(s + 1) * P], a_rows[:, s, :], ident[:, :])
                    last.then_inc(xn_turned, 1)
                    pe.wait_ge(xnT_ready, b + 1)
                    for n, (what, w) in enumerate(UNITS):
                        if n >= 4:
                            taken = odd_taken if n % 2 else even_taken
                            pe.wait_ge(taken, b * HALF + (n - 4) // 2 + 1)
                        if what == "v":
                            s, half = w // 2, w % 2
                            last = nc.tensor.matmul(bank[n % 4][:, :], a_xnT[:, s * P:(s + 1) * P],
                                                    wv_s[:, half * 512:(half + 1) * 512], start=True, stop=True)
                        else:
                            src = wq_s if what == "q" else wk_s
                            for m in range(2):
                                p = 2 * w + m
                                last = nc.tensor.matmul(bank[n % 4][:, m * SEQ:(m + 1) * SEQ], src[:, p * P:(p + 1) * P],
                                                        a_xnT[:, :], start=True, stop=True)
                        last.then_inc(qkv_done, 1)

                    def scores(p):
                        if p >= 2:
                            pe.wait_ge(exp_done, b * HEADS + 2 * p - 2)
                        for qt in range(2):
                            for hh in range(2):
                                r = DH * hh
                                last = nc.tensor.matmul(score_ps(2 * p + hh)[:, qt * SEQ:(qt + 1) * SEQ],
                                                        qT[r:r + DH, p, qt * P:(qt + 1) * P], kT[r:r + DH, p, :],
                                                        start=True, stop=True)
                        last.then_inc(scores_done, 1)

                    def turn(h):
                        pe.wait_ge(scaled, b * HEADS + h + 1)
                        if h >= 2:
                            pe.wait_ge(probT_ready, b * HEADS + h - 1)
                        for kt in range(2):
                            for qt in range(2):
                                last = nc.tensor.transpose(turn_ps[h % 2][:, kt * SEQ + qt * P:kt * SEQ + (qt + 1) * P],
                                                           prob[:, h % 3, qt, kt * P:(kt + 1) * P], ident[:, :])
                        last.then_inc(prob_turned, 1)

                    def context(p):
                        pe.wait_ge(probT_ready, b * HEADS + 2 * p + 2)
                        if p >= 1:
                            pe.wait_ge(ctxT_ready, b * PAIRS + p)
                        for kt in range(2):
                            for hh in range(2):
                                r, h = DH * hh, 2 * p + hh
                                last = nc.tensor.matmul(ctx_ps[r:r + DH, 0:SEQ], v_s[:, kt, h * DH:(h + 1) * DH],
                                                        probT[:, h % 4, kt, :], start=(kt == 0), stop=(kt == 1))
                        last.then_inc(context_done, 1)

                    pe.wait_ge(even_taken, b * HALF + HALF)
                    pe.wait_ge(odd_taken, b * HALF + HALF)
                    scores(0)
                    scores(1)
                    for p in range(PAIRS):
                        turn(2 * p)
                        turn(2 * p + 1)
                        if p + 2 < PAIRS:
                            scores(p + 2)
                        if p >= 1:
                            context(p - 1)
                    context(PAIRS - 1)
                    pe.wait_ge(ctxT_ready, b * PAIRS + PAIRS)
                    for p in range(PAIRS):
                        last = nc.tensor.matmul(aux[:, 0:SEQ], wo_s[:, p, :], ctxT[:, p, :], start=(p == 0), stop=(p == PAIRS - 1))
                    last.then_inc(out_done, 1)
                    pe.wait_ge(outT_ready, b + 1)
                    for s in range(2):
                        last = nc.tensor.transpose(aux[:, SEQ + s * P:SEQ + (s + 1) * P], a_yT[:, s * P:(s + 1) * P], ident[:, :])
                    last.then_inc(out_turned, 1)

            def take(engine, b, n, ready):
                what, w = UNITS[n]
                engine.wait_ge(qkv_done, b * len(UNITS) + n + 1)
                if what == "v":
                    s, half = w // 2, w % 2
                    dst = v_s[:, s, half * 512:(half + 1) * 512]
                else:
                    dst = (qT if what == "q" else kT)[:, 2 * w:2 * w + 2, :].rearrange("p m q -> p (m q)")
                if n % 2:
                    nc.vector.tensor_copy(dst, bank[n % 4][:, :]).then_inc(ready, 1)
                else:
                    nc.scalar.activation(dst, bank[n % 4][:, :], ACT.Copy, scale=DH ** -0.5 if what == "q" else 1.0).then_inc(ready, 1)

            @block.scalar
            def _(act):
                with act.Fori(0, BATCH) as b:
                    for n in range(0, len(UNITS), 2):
                        take(act, b, n, even_taken)

                    def exps(h):
                        act.wait_ge(max_done, b * HEADS + h + 1)
                        if h >= 3:
                            act.wait_ge(prob_turned, b * HEADS + h - 2)
                        for qt in range(2):
                            last = nc.scalar.activation(prob[:, h % 3, qt, :], score_ps(h)[:, qt * SEQ:(qt + 1) * SEQ], ACT.Exp,
                                                        bias=neg_max[:, h, qt:qt + 1], accum_out=row_sum[:, h, qt:qt + 1])
                        last.then_inc(exp_done, 1)

                    def take_turned(h):
                        act.wait_ge(prob_turned, b * HEADS + h + 1)
                        if h >= 4:
                            act.wait_ge(context_done, b * PAIRS + (h - 4) // 2 + 1)
                        nc.scalar.activation(probT[:, h % 4, :, :].rearrange("p k q -> p (k q)"), turn_ps[h % 2][:, :],
                                             ACT.Copy).then_inc(probT_ready, 1)

                    for h in range(HEADS + 2):
                        if h < HEADS:
                            exps(h)
                        if h >= 2:
                            take_turned(h - 2)
                    act.wait_ge(out_done, b + 1)
                    nc.scalar.activation(a_yT[:, :], aux[:, 0:SEQ], ACT.Identity, bias=bias_o[:, 0:1]).then_inc(outT_ready, 1)

            @block.vector
            def _(dve):
                CHAIN = 2 + HEADS
                with dve.Fori(0, BATCH) as b:
                    def step(ins, n):
                        ins.then_inc(chain, 1)
                        dve.wait_ge(chain, b * CHAIN + n)

                    def row(s):
                        return xs[:, bass.ds(2 * b + s, 1), :].rearrange("p a d -> p (a d)")
                    for s in range(2):
                        last = nc.vector.bn_stats(stats[:, s, :], row(s))
                    step(last, 1)
                    nc.vector.memset(spare[:, :], 0.0)
                    for s in range(2):
                        last = nc.vector.bn_aggr(mean_var[:, s, :], stats[:, s, :])
                    step(last, 2)
                    nc.vector.tensor_scalar(var_eps[:, 0:2], mean_var[:, 0:2, 1], LN_EPS, None, ALU.add).then_inc(var_ready, 1)
                    dve.wait_ge(rstd_ready, b + 1)
                    for s in range(2):
                        last = nc.vector.tensor_scalar(a_rows[:, s, :], row(s), mean_var[:, s, 0:1], rstd[:, s:s + 1],
                                                       ALU.subtract, ALU.mult)
                    last.then_inc(xn_ready, 1)
                    dve.wait_ge(xn_turned, b + 1)
                    nc.vector.tensor_copy(a_xnT[:, :], aux[:, 0:SEQ]).then_inc(xnT_ready, 1)
                    for n in range(1, len(UNITS), 2):
                        take(dve, b, n, odd_taken)

                    def maxes(h):
                        if h % 2 == 0:
                            dve.wait_ge(scores_done, b * PAIRS + h // 2 + 1)
                        nc.vector.tensor_reduce(neg_max[:, h, :], score_ps(h)[:, :].rearrange("p (t k) -> p t k", k=SEQ),
                                                AX.X, ALU.max, negate=True).then_inc(max_done, 1)

                    def scale(h):
                        dve.wait_ge(exp_done, b * HEADS + h + 1)
                        step(nc.vector.tensor_scalar(row_inv[:, h, :], row_sum[:, h, :], SOFTMAX_EPS, None, ALU.add), 3 + h)
                        nc.vector.reciprocal(row_inv[:, h, :], row_inv[:, h, :]).then_inc(inv_ready, 1)
                        dve.wait_ge(inv_ready, b * HEADS + h + 1)
                        for qt in range(2):
                            last = nc.vector.tensor_scalar(prob[:, h % 3, qt, :], prob[:, h % 3, qt, :], row_inv[:, h, qt:qt + 1],
                                                           None, ALU.mult)
                        last.then_inc(scaled, 1)

                    def take_context(p):
                        dve.wait_ge(context_done, b * PAIRS + p + 1)
                        nc.vector.tensor_copy(ctxT[:, p, :], ctx_ps[:, 0:SEQ]).then_inc(ctxT_ready, 1)

                    maxes(0)
                    maxes(1)
                    for h in range(HEADS):
                        scale(h)
                        if h + 2 < HEADS:
                            maxes(h + 2)
                        if h % 2 == 1 and h >= 5:
                            take_context((h - 5) // 2)
                    for p in range(PAIRS - 2, PAIRS):
                        take_context(p)
                    dve.wait_ge(out_turned, b + 1)
                    here = xs[:, bass.ds(2 * b, 2), :]
                    nc.vector.tensor_tensor(here, here, aux[:, SEQ:2 * SEQ].rearrange("p (s d) -> p s d", d=D),
                                            ALU.add).then_inc(added, 1)
                    dve.wait_ge(added, b + 1)

        with nc.Block() as block:
            feed_forward(block, 0, [(gate_proj, gate_hi, gate_lo), (up_proj, up_hi, up_lo), (down_proj, down_hi, down_lo)])
        with nc.Block() as block:
            attention(block)
        with nc.Block() as block:
            feed_forward(block, 1, [(down_proj, down_hi, down_lo)])


_SHAPE = (16, 256, 128)


def kernel(**inputs):
    import numpy as _np
    import concourse.bacc as _bacc
    from concourse import mybir as _mybir
    from concourse.bass_utils import run_bass_kernel_spmd as _run

    a = {k[3:]: _np.asarray(v) for k, v in inputs.items()}
    def columns(w):
        w = w.reshape(GROUPS, GE, D, CPG, FS).transpose(2, 0, 3, 1, 4)
        return w.reshape(D, GROUPS, GW)
    down = a["ffn_down_proj"].reshape(GROUPS, GE, CPG, FS, D).transpose(1, 3, 0, 2, 4).reshape(P, GROUPS, GW)
    laid = {
        "x": a["attn_x"],
        "wq": a["attn_Wq"].T, "wk": a["attn_Wk"].T, "wv": a["attn_Wv"].T,
        "wo": a["attn_Wo"].T.reshape(PAIRS, P, D).transpose(1, 0, 2),
        "bo": a["attn_bo"].reshape(D, 1),
        "gate_w": a["ffn_gate_w"].T,
        "gate_proj": columns(a["ffn_gate_proj"]), "up_proj": columns(a["ffn_up_proj"]), "down_proj": down,
    }
    nc = _bacc.Bacc("TRN2", target_bir_lowering=False, num_devices=1)
    arrays, args = {}, {}
    for name, v in laid.items():
        arrays[f"in_{name}"] = v = _np.ascontiguousarray(v)
        args[name] = nc.dram_tensor(f"in_{name}", v.shape, _mybir.dt.from_np(v.dtype), kind="ExternalInput").ap()
    args["out"] = nc.dram_tensor("out_x", _SHAPE, _mybir.dt.float32, kind="ExternalOutput").ap()
    macaron_block(nc, **args)
    r = _run(nc, [arrays], core_ids=[0])
    return r.results[0]["out_x"]
```

```python
import concourse.bass as bass
from concourse import mybir
from contextlib import ExitStack

FP32 = mybir.dt.float32
FP32R = mybir.dt.float32r
ALU = mybir.AluOpType
ACT = mybir.ActivationFunctionType
AX = mybir.AxisListType

P = 128
D = 128
BATCH, SEQ = 16, 256
E, F, TOP_K = 64, 96, 8
HEADS, DH = 16, 64
INNER = HEADS * DH
LN_EPS, SOFTMAX_EPS = 1e-5, 1e-10

TILES = BATCH * SEQ // P
BT = 4
NB = BT * P
BLOCKS = TILES // BT
GE = 4
GROUPS = E // GE
FS = P // GE
CPG = F // FS
CHUNKS = GROUPS * CPG
GW = CPG * P
UNROLL = 2
LAG = 3
PAIR_CHUNKS = UNROLL * CHUNKS

STATS_AT, NORM_AT, TURN_AT, SPLIT_AT, LOGIT_AT, SHIFT_AT = 3, 6, 9, 11, 14, 17
EXP_AT, PROB_AT, TOP_AT, PICK_AT, WEIGHT_AT, WTURN_AT, WCOPY_AT = 19, 22, 25, 28, 31, 34, 36

PAIRS = HEADS // 2


def macaron_block(nc, x, wq, wk, wv, wo, bo, gate_w, gate_proj, up_proj, down_proj, out):
    x_v = x.rearrange("b (p s) d -> p b (s d)", s=2)
    out_v = out.rearrange("b (p s) d -> p b (s d)", s=2)

    ctx = ExitStack()
    with ctx:
        def sb(name, shape, dt=FP32, scope=ctx):
            return scope.enter_context(nc.sbuf_tensor(name, shape, dt))

        def sem(name):
            return ctx.enter_context(nc.semaphore(name))

        gate_hi = sb("gate_hi", [P, GROUPS, GW], FP32R)
        gate_lo = sb("gate_lo", [P, GROUPS, GW], FP32R)
        up_hi = sb("up_hi", [P, GROUPS, GW], FP32R)
        up_lo = sb("up_lo", [P, GROUPS, GW], FP32R)
        xs = sb("xs", [P, TILES + BT, D])
        spread = sb("spread", [P, GROUPS, P], FP32R)
        ident = sb("ident", [P, P])
        rw = sb("rw", [P, E])
        rw_hi = sb("rw_hi", [P, E], FP32R)
        rw_lo = sb("rw_lo", [P, E], FP32R)
        bias_row = sb("bias_row", [1, D])
        ones_row = sb("ones_row", [1, P])
        stats = sb("stats", [P, BT, 6])
        mean_var = sb("mean_var", [P, BT, 2])
        var_eps = sb("var_eps", [P, BT])
        rstd = sb("rstd", [P, BT])
        neg_half = sb("neg_half", [P, BT])
        spare = sb("spare", [P, 1])

        with ExitStack() as ffn_scope:
            def fb(name, shape, dt=FP32):
                return sb(name, shape, dt, ffn_scope)
            down_hi = fb("down_hi", [P, GROUPS, GW], FP32R)
            down_lo = fb("down_lo", [P, GROUPS, GW], FP32R)
            act_buf = fb("act_buf", [P, 3, NB])
            h_hi = fb("h_hi", [P, LAG, NB], FP32R)
            h_lo = fb("h_lo", [P, LAG, NB], FP32R)
            xnT_hi = fb("xnT_hi", [P, 2, NB], FP32R)
            xnT_lo = fb("xnT_lo", [P, 2, NB], FP32R)
            wT = fb("wT", [P, 2, NB], FP32R)
            rows = fb("rows", [P, BT, D])
            yT = rows[:, :, :].rearrange("p t d -> p (t d)")
            probs = fb("probs", [P, BT, E])
            rest = fb("rest", [P, BT, E])
            best = fb("best", [P, BT, TOP_K])
            col = fb("col", [P, 6, BT])

        with ExitStack() as attn_scope:
            def ab(name, shape, dt=FP32):
                return sb(name, shape, dt, attn_scope)
            wq_s = ab("wq_s", [P, INNER])
            wk_s = ab("wk_s", [P, INNER])
            wv_s = ab("wv_s", [P, INNER])
            wo_s = ab("wo_s", [P, PAIRS, D])
            qkT = ab("qkT", [P, PAIRS, 2, SEQ])
            v_s = ab("v_s", [P, 2, INNER])
            prob = ab("prob", [P, 8, 2, SEQ])
            probT = ab("probT", [P, 4, 2, SEQ])
            ctxT = ab("ctxT", [P, PAIRS, SEQ])
            a_rows = ab("a_rows", [P, 2, D])
            a_xnT = ab("a_xnT", [P, SEQ])
            neg_max = ab("neg_max", [P, HEADS, 2])
            row_sum = ab("row_sum", [P, HEADS, 2])
            row_inv = ab("row_inv", [P, HEADS, 2])

        bank = [ctx.enter_context(nc.psum_tensor(f"bank{i}", [P, 512], FP32)) for i in range(8)]

        consts = sem("consts")
        x_in = sem("x_in")
        x_out = sem("x_out")
        small_in = sem("small_in")
        rw_split = sem("rw_split")

        def feed_forward(block, ph, loads):
            def s(name):
                return sem(f"{name}{ph}")
            stage_in = [s(f"stage_in{k}_") for k in range(3)]
            stage_hi, stage_lo = s("stage_hi"), s("stage_lo")
            chain = s("chain")
            var_ready, rstd_ready, xn_ready = s("var_ready"), s("rstd_ready"), s("xn_ready")
            xn_turned, xnT_ready = s("xn_turned"), s("xnT_ready")
            logits_done, shifted, exp_done = s("logits_done"), s("shifted"), s("exp_done")
            weights_ready, weights_turned, wT_ready = s("weights_ready"), s("weights_turned"), s("wT_ready")
            spread_done, gate_done, up_done = s("spread_done"), s("gate_done"), s("up_done")
            silu_done, scaled, h_done = s("silu_done"), s("scaled"), s("h_done")
            hi_done, lo_done, down_done = s("hi_done"), s("lo_done"), s("down_done")
            yT_done, y_turned, x_added = s("yT_done"), s("y_turned"), s("x_added")

            gate_ps, up_ps, w_ps = bank[0:2], bank[2:5], bank[5]
            y_ps, aux = bank[6], bank[7]
            LOADS = [(v[:, g, :], hi[:, g, :], lo[:, g, :]) for g in range(GROUPS) for v, hi, lo in loads]

            def positions():
                for c in range(PAIR_CHUNKS + LAG):
                    yield c, c // CHUNKS, c % CHUNKS

            @block.sync
            def _(sp):
                if ph == 0:
                    sp.dma_start(xs[:, 0:BT, :].rearrange("p (b s) d -> p b (s d)", s=2), x_v[:, 0:2, :]).then_inc(x_in, 16)
                for n, (view, _hi, _lo) in enumerate(LOADS):
                    if n >= 3:
                        sp.wait_ge(stage_lo, n - 2)
                    sp.dma_start(act_buf[:, n % 3, 0:GW], view).then_inc(stage_in[n % 3], 16)
                if ph == 1:
                    with sp.Fori(0, BLOCKS) as i:
                        sp.wait_ge(x_added, i + 1)
                        sp.dma_start(out_v[:, bass.ds(2 * i, 2), :],
                                     xs[:, bass.ds(BT * i, BT), :].rearrange("p (b s) d -> p b (s d)", s=2)).then_inc(x_out, 16)
                    sp.wait_ge(x_out, 16 * BLOCKS)

            @block.gpsimd
            def _(pool):
                if ph == 0:
                    nc.gpsimd.memset(ident[:, :], 0.0).then_inc(consts, 1)
                    nc.gpsimd.memset(spread[:, :, :].bitcast(FP32), 0.0).then_inc(consts, 1)
                    nc.gpsimd.memset(neg_half[:, :], -0.5).then_inc(consts, 1)
                    nc.gpsimd.memset(xs[:, TILES:TILES + BT, :], 0.0).then_inc(consts, 1)
                    pool.wait_ge(consts, 4)
                    nc.gpsimd.affine_select(out=ident[:, :], in_=ident[:, :], compare_op=ALU.not_equal, fill=1.0,
                                            base=0, pattern=[[-1, P]], channel_multiplier=1).then_inc(consts, 1)
                    wide = spread[:, :, :].rearrange("p g (i k) -> p (g i) k", k=FS)
                    nc.gpsimd.affine_select(out=wide, in_=wide.bitcast(FP32), compare_op=ALU.not_equal, fill=1.0,
                                            base=0, pattern=[[-1, E], [0, FS]], channel_multiplier=1).then_inc(consts, 1)
                    pool.wait_ge(consts, 6)
                    nc.gpsimd.affine_select(out=wide, in_=wide.bitcast(FP32), compare_op=ALU.not_equal, fill=1.0,
                                            base=-E, pattern=[[-1, E], [0, FS]], channel_multiplier=1).then_inc(consts, 1)

                def rstd_of(count):
                    pool.wait_ge(var_ready, count)
                    nc.gpsimd.tensor_tensor(rstd[:, :], var_eps[:, :], neg_half[:, :], ALU.pow).then_inc(rstd_ready, 1)

                rstd_of(1)
                with pool.Fori(0, BLOCKS // UNROLL) as i:
                    for c, blk, k in positions():
                        if c < PAIR_CHUNKS and k == STATS_AT:
                            rstd_of(i * UNROLL + blk + 2)
                        if c < PAIR_CHUNKS:
                            pool.wait_ge(hi_done, i * PAIR_CHUNKS + c + 1)
                            if c >= LAG:
                                pool.wait_ge(down_done, i * PAIR_CHUNKS + c - LAG + 1)
                            nc.gpsimd.tensor_tensor(h_lo[:, c % LAG, :], act_buf[:, c % 3, :], h_hi[:, c % LAG, :].bitcast(FP32),
                                                    ALU.subtract).then_inc(lo_done, 1)

            @block.scalar
            def _(act):
                if ph == 0:
                    act.dma_start(rw[:, :], gate_w).then_inc(small_in, 16)
                    act.dma_start(xs[:, BT:TILES, :].rearrange("p (b s) d -> p b (s d)", s=2), x_v[:, 2:BATCH, :]).then_inc(x_in, 16)

                for n, (_view, hi, _lo) in enumerate(LOADS):
                    act.wait_ge(stage_in[n % 3], 16 * (n // 3 + 1))
                    nc.scalar.activation(hi, act_buf[:, n % 3, 0:GW], ACT.Copy).then_inc(stage_hi, 1)

                def exp_of(count):
                    act.wait_ge(shifted, count)
                    nc.scalar.activation(probs[:, :, :], rest[:, :, :], ACT.Exp).then_inc(exp_done, 1)

                def take_yT(down):
                    act.wait_ge(down_done, down)
                    nc.scalar.activation(yT[:, :], y_ps[:, :], ACT.Copy).then_inc(yT_done, 1)

                exp_of(1)
                with act.Fori(0, BLOCKS // UNROLL) as i:
                    for c, blk, k in positions():
                        if c < PAIR_CHUNKS:
                            act.wait_ge(gate_done, i * PAIR_CHUNKS + c + 1)
                            if c >= 3:
                                act.wait_ge(lo_done, i * PAIR_CHUNKS + c - 2)
                            nc.scalar.activation(act_buf[:, c % 3, :], gate_ps[c % 2][:, :], ACT.Silu).then_inc(silu_done, 1)
                        if 1 <= c <= PAIR_CHUNKS:
                            act.wait_ge(h_done, i * PAIR_CHUNKS + c)
                            if c - 1 >= LAG:
                                act.wait_ge(down_done, i * PAIR_CHUNKS + c - LAG)
                            nc.scalar.activation(h_hi[:, (c - 1) % LAG, :], act_buf[:, (c - 1) % 3, :], ACT.Copy).then_inc(hi_done, 1)
                        if c == CHUNKS + LAG:
                            take_yT(i * PAIR_CHUNKS + CHUNKS)
                        if c < PAIR_CHUNKS and k == EXP_AT:
                            exp_of(i * UNROLL + blk + 2)
                    take_yT(i * PAIR_CHUNKS + PAIR_CHUNKS)

            @block.tensor
            def _(pe):
                def split_product(ps, hi, lo, m_hi, m_lo, start, stop):
                    nc.tensor.matmul(ps, hi, m_hi, start=start, stop=False)
                    nc.tensor.matmul(ps, hi, m_lo, start=False, stop=False)
                    return nc.tensor.matmul(ps, lo, m_hi, start=False, stop=stop)

                def turn_rows(ready, count, done):
                    pe.wait_ge(ready, count)
                    for t in range(BT):
                        last = nc.tensor.transpose(aux[:, t * P:(t + 1) * P], rows[:, t, :], ident[:, :])
                    last.then_inc(done, 1)

                def logits(count, slot):
                    pe.wait_ge(xnT_ready, count)
                    for t in range(BT):
                        a, b = t * P, (t + 1) * P
                        last = split_product(aux[:, t * E:(t + 1) * E], xnT_hi[:, slot, a:b], xnT_lo[:, slot, a:b],
                                             rw_hi[:, :], rw_lo[:, :], True, True)
                    last.then_inc(logits_done, 1)

                def turn_y(count, routings):
                    pe.wait_ge(yT_done, count)
                    pe.wait_ge(wT_ready, routings)
                    for t in range(BT):
                        last = nc.tensor.transpose(aux[:, t * P:(t + 1) * P], yT[:, t * P:(t + 1) * P], ident[:, :])
                    last.then_inc(y_turned, 1)

                pe.wait_ge(consts, 7)
                pe.wait_ge(rw_split, 2)
                turn_rows(xn_ready, 1, xn_turned)
                logits(1, 0)
                turn_rows(weights_ready, 2, weights_turned)
                pe.wait_ge(stage_lo, len(LOADS))
                with pe.Fori(0, BLOCKS // UNROLL) as i:
                    for c, blk, k in positions():
                        if c < PAIR_CHUNKS:
                            G, j = k // CPG, k % CPG
                            a, b = j * P, (j + 1) * P
                            if k == 0:
                                pe.wait_ge(xnT_ready, i * UNROLL + blk + 1)
                            if c >= 2:
                                pe.wait_ge(silu_done, i * PAIR_CHUNKS + c - 1)
                            split_product(gate_ps[c % 2][:, :], gate_hi[:, G, a:b], gate_lo[:, G, a:b],
                                          xnT_hi[:, blk, :], xnT_lo[:, blk, :], True, True).then_inc(gate_done, 1)
                            if c >= 3:
                                pe.wait_ge(h_done, i * PAIR_CHUNKS + c - 2)
                            split_product(up_ps[c % 3][:, :], up_hi[:, G, a:b], up_lo[:, G, a:b],
                                          xnT_hi[:, blk, :], xnT_lo[:, blk, :], True, True).then_inc(up_done, 1)
                            if j == 0:
                                if k == 0:
                                    pe.wait_ge(wT_ready, i * UNROLL + blk + 1)
                                if c >= 1:
                                    pe.wait_ge(scaled, i * PAIR_CHUNKS + c)
                                nc.tensor.matmul(w_ps[:, :], spread[:, G, :], wT[:, blk, :],
                                                 start=True, stop=True).then_inc(spread_done, 1)
                        if c >= LAG:
                            d = c - LAG
                            kd = d % CHUNKS
                            G, a, b = kd // CPG, (kd % CPG) * P, (kd % CPG + 1) * P
                            pe.wait_ge(lo_done, i * PAIR_CHUNKS + d + 1)
                            if kd == 0 and d > 0:
                                pe.wait_ge(yT_done, i * UNROLL + 1)
                            split_product(y_ps[:, :], down_hi[:, G, a:b], down_lo[:, G, a:b],
                                          h_hi[:, d % LAG, :], h_lo[:, d % LAG, :], kd == 0, kd == CHUNKS - 1).then_inc(down_done, 1)
                        if c == CHUNKS + LAG:
                            turn_y(i * UNROLL + 1, i * UNROLL + 2)
                        if c < PAIR_CHUNKS:
                            nxt = i * UNROLL + blk + 2
                            if k == TURN_AT:
                                turn_rows(xn_ready, nxt, xn_turned)
                            if k == LOGIT_AT:
                                logits(nxt, 1 - blk)
                            if k == WTURN_AT:
                                turn_rows(weights_ready, 2 * nxt, weights_turned)
                    turn_y(i * UNROLL + 2, i * UNROLL + 3)

            @block.vector
            def _(dve):
                if ph == 0:
                    dve.wait_ge(small_in, 16)
                    nc.vector.tensor_copy(rw_hi[:, :], rw[:, :]).then_inc(rw_split, 1)
                    dve.wait_ge(rw_split, 1)
                    nc.vector.tensor_tensor(rw_lo[:, :], rw[:, :], rw_hi[:, :].bitcast(FP32), ALU.subtract).then_inc(rw_split, 1)
                    dve.wait_ge(x_in, 32)
                    dve.wait_ge(consts, 7)

                CHAIN = 2 + 5 + 7
                def over_experts(a):
                    return a.unsqueeze(2).broadcast_to([P, BT, E])

                def stage(k, tile0, done, nth, slot):
                    def step(ins, n):
                        ins.then_inc(chain, 1)
                        dve.wait_ge(chain, done + n)
                    if k == STATS_AT:
                        for t in range(BT):
                            last = nc.vector.bn_stats(stats[:, t, :], xs[:, bass.ds(tile0 + t, 1), :].rearrange("p a d -> p (a d)"))
                        step(last, 1)
                        nc.vector.memset(spare[:, :], 0.0)
                        for t in range(BT):
                            last = nc.vector.bn_aggr(mean_var[:, t, :], stats[:, t, :])
                        step(last, 2)
                        nc.vector.tensor_scalar(var_eps[:, :], mean_var[:, :, 1], LN_EPS, None, ALU.add).then_inc(var_ready, 1)
                    if k == NORM_AT:
                        dve.wait_ge(rstd_ready, nth)
                        for t in range(BT):
                            last = nc.vector.tensor_scalar(rows[:, t, :], xs[:, bass.ds(tile0 + t, 1), :].rearrange("p a d -> p (a d)"),
                                                           mean_var[:, t, 0:1], rstd[:, t:t + 1], ALU.subtract, ALU.mult)
                        last.then_inc(xn_ready, 1)
                    if k == SPLIT_AT:
                        dve.wait_ge(xn_turned, nth)
                        step(nc.vector.tensor_copy(xnT_hi[:, slot, :], aux[:, :]), 3)
                        nc.vector.tensor_tensor(xnT_lo[:, slot, :], aux[:, :], xnT_hi[:, slot, :].bitcast(FP32),
                                                ALU.subtract).then_inc(xnT_ready, 1)
                    lg = aux[:, 0:BT * E].rearrange("p (t e) -> p t e", e=E)
                    if k == SHIFT_AT:
                        dve.wait_ge(logits_done, nth)
                        step(nc.vector.tensor_reduce(col[:, 0, :], lg, AX.X, ALU.max), 4)
                        nc.vector.tensor_tensor(rest[:, :, :], lg, over_experts(col[:, 0, :]), ALU.subtract).then_inc(shifted, 1)
                    if k == PROB_AT:
                        dve.wait_ge(exp_done, nth)
                        step(nc.vector.tensor_reduce(col[:, 1, :], probs[:, :, :], AX.X, ALU.add), 5)
                        step(nc.vector.reciprocal(col[:, 2, :], col[:, 1, :]), 6)
                        nc.vector.tensor_tensor(probs[:, :, :], probs[:, :, :], over_experts(col[:, 2, :]), ALU.mult).then_inc(chain, 1)
                    if k == TOP_AT:
                        dve.wait_ge(chain, done + 7)
                        nc.vector.memset(spare[:, :], 0.0)
                        for t in range(BT):
                            last = nc.vector.max(best[:, t, :], probs[:, t, :])
                        last.then_inc(chain, 1)
                    if k == PICK_AT:
                        dve.wait_ge(chain, done + 8)
                        nc.vector.memset(spare[:, :], 0.0)
                        for t in range(BT):
                            last = nc.vector.match_replace(rest[:, t, :], best[:, t, :], probs[:, t, :], -1.0)
                        step(last, 9)
                        step(nc.vector.tensor_reduce(col[:, 3, :], best[:, :, :], AX.X, ALU.add), 10)
                        step(nc.vector.reciprocal(col[:, 4, :], col[:, 3, :]), 11)
                    if k == WEIGHT_AT:
                        step(nc.vector.tensor_scalar(col[:, 5, :], col[:, 4, :], -0.5, None, ALU.mult), 12)
                        step(nc.vector.scalar_tensor_tensor(out=rest[:, :, :], in0=rest[:, :, :], scalar=0.0, in1=probs[:, :, :],
                                                            op0=ALU.max, op1=ALU.subtract), 13)
                        nc.vector.tensor_tensor(probs[:, :, :], rest[:, :, :], over_experts(col[:, 5, :]), ALU.mult).then_inc(chain, 1)
                        dve.wait_ge(chain, done + CHAIN)
                        hi = rows[:, :, 0:E].bitcast(FP32R)
                        nc.vector.tensor_copy(hi, probs[:, :, :]).then_inc(weights_ready, 1)
                        dve.wait_ge(weights_ready, 2 * nth - 1)
                        nc.vector.tensor_tensor(rows[:, :, E:2 * E].bitcast(FP32R), probs[:, :, :], rows[:, :, 0:E],
                                                ALU.subtract).then_inc(weights_ready, 1)
                    if k == WCOPY_AT:
                        dve.wait_ge(weights_turned, nth)
                        nc.vector.tensor_copy(wT[:, slot, :], aux[:, :]).then_inc(wT_ready, 1)

                STAGES = (STATS_AT, NORM_AT, SPLIT_AT, SHIFT_AT, PROB_AT, TOP_AT, PICK_AT, WEIGHT_AT, WCOPY_AT)

                def add_y(count, tile0):
                    dve.wait_ge(y_turned, count)
                    here = xs[:, bass.ds(tile0, BT), :]
                    nc.vector.tensor_tensor(here, here, aux[:, :].rearrange("p (t d) -> p t d", d=D), ALU.add).then_inc(x_added, 1)

                def low_part(n):
                    _view, hi, lo = LOADS[n]
                    dve.wait_ge(stage_hi, n + 1)
                    nc.vector.tensor_tensor(lo, act_buf[:, n % 3, 0:GW], hi.bitcast(FP32), ALU.subtract).then_inc(stage_lo, 1)

                for n in range(len(LOADS)):
                    low_part(n)
                for k in STAGES:
                    stage(k, 0, 0, 1, 0)
                with dve.Fori(0, BLOCKS // UNROLL) as i:
                    for c, blk, k in positions():
                        if c < PAIR_CHUNKS:
                            at = i * PAIR_CHUNKS + c + 1
                            G = c // CPG
                            buf = act_buf[:, c % 3, :]
                            dve.wait_ge(silu_done, at)
                            if c % CPG == 0:
                                dve.wait_ge(spread_done, i * (PAIR_CHUNKS // CPG) + G + 1)
                            nc.vector.tensor_tensor(buf, buf, w_ps[:, :], ALU.mult).then_inc(scaled, 1)
                            dve.wait_ge(scaled, at)
                            dve.wait_ge(up_done, at)
                            nc.vector.tensor_tensor(buf, buf, up_ps[c % 3][:, :], ALU.mult).then_inc(h_done, 1)
                            if k in STAGES:
                                nth = i * UNROLL + blk + 2
                                stage(k, (i * UNROLL + blk + 1) * BT, (i * UNROLL + blk + 1) * CHAIN, nth, 1 - blk)
                        if c == CHUNKS + LAG:
                            add_y(i * UNROLL + 1, i * UNROLL * BT)
                    add_y(i * UNROLL + 2, (i * UNROLL + 1) * BT)


        def attention(block):
            weights_in, q_scaled = sem("attn_weights_in"), sem("q_scaled")
            chain, var_ready, rstd_ready, xn_ready = sem("a_chain"), sem("a_var_ready"), sem("a_rstd_ready"), sem("a_xn_ready")
            xn_turned, xnT_ready, unit_done = sem("a_xn_turned"), sem("a_xnT_ready"), sem("unit_done")
            unit_taken = sem("unit_taken")
            scores_done, max_done, exp_done, sum_ready, inv_ready, scaled = (
                sem("scores_done"), sem("max_done"), sem("a_exp_done"), sem("sum_ready"), sem("inv_ready"), sem("a_scaled"))
            prob_turned, probT_ready, context_done, ctxT_ready = (sem("prob_turned"), sem("probT_ready"),
                                                                  sem("context_done"), sem("ctxT_ready"))
            out_done, added = sem("out_done"), sem("a_added")

            turn_ps, unit_ps, ctx_ps, out_ps = bank[4:8]
            UNITS = ([("qk", p) for p in range(6)] + [("v", (0, 0)), ("qk", 6), ("v", (1, 0)), ("qk", 7),
                                                       ("v", (0, 1)), ("v", (1, 1))])
            NU = len(UNITS)
            AHEAD = 4
            EXP_AHEAD = 3
            SCALED_AHEAD = 2

            def score_ps(h):
                return bank[h % 4]

            def later(b, h):
                return (b, h) if h < HEADS else (b + 1, h - HEADS)

            @block.sync
            def _(sp):
                for a, b in ((wq_s[:, :], wq), (wk_s[:, :], wk), (wv_s[:, :], wv), (wo_s[:, :, :], wo)):
                    sp.dma_start(a, b).then_inc(weights_in, 16)
                sp.dma_start(bias_row[:, :], bo).then_inc(weights_in, 16)

            @block.gpsimd
            def _(pool):
                nc.gpsimd.memset(ones_row[:, :], 1.0).then_inc(q_scaled, 1)
                pool.wait_ge(weights_in, 16 * 5)
                nc.gpsimd.tensor_scalar(wq_s[:, :], wq_s[:, :], DH ** -0.5, None, ALU.mult).then_inc(q_scaled, 1)

                def rstd_of(n):
                    pool.wait_ge(var_ready, n + 1)
                    nc.gpsimd.tensor_tensor(rstd[:, 0:2], var_eps[:, 0:2], neg_half[:, 0:2], ALU.pow).then_inc(rstd_ready, 1)
                rstd_of(0)
                rstd_of(1)
                with pool.Fori(0, BATCH) as b:
                    rstd_of(b + 2)

            @block.tensor
            def _(pe):
                def turn_xn(n, first):
                    pe.wait_ge(xn_ready, n + 1)
                    if not first:
                        pe.wait_ge(unit_taken, n * NU)
                    for s in range(2):
                        last = nc.tensor.transpose(unit_ps[:, s * P:(s + 1) * P], a_rows[:, s, :], ident[:, :])
                    last.then_inc(xn_turned, 1)

                def unit(n, u):
                    what, w = UNITS[u]
                    if u == 0:
                        pe.wait_ge(xnT_ready, n + 1)
                    else:
                        pe.wait_ge(unit_taken, n * NU + u)
                    if what == "v":
                        s, half = w
                        last = nc.tensor.matmul(unit_ps[:, :], a_xnT[:, s * P:(s + 1) * P],
                                                wv_s[:, half * 512:(half + 1) * 512], start=True, stop=True)
                    else:
                        for m, weights in enumerate((wq_s, wk_s)):
                            last = nc.tensor.matmul(unit_ps[:, m * SEQ:(m + 1) * SEQ], weights[:, w * P:(w + 1) * P],
                                                    a_xnT[:, :], start=True, stop=True)
                    last.then_inc(unit_done, 1)

                def scores(n, p, first=False):
                    pe.wait_ge(unit_taken, n * NU + UNITS.index(("qk", p)) + 1)
                    if not first:
                        pe.wait_ge(exp_done, n * HEADS + 2 * p - 2)
                    for qt in range(2):
                        for hh in range(2):
                            r = DH * hh
                            last = nc.tensor.matmul(score_ps(2 * p + hh)[:, qt * SEQ:(qt + 1) * SEQ],
                                                    qkT[r:r + DH, p, 0, qt * P:(qt + 1) * P], qkT[r:r + DH, p, 1, :],
                                                    start=True, stop=True)
                    last.then_inc(scores_done, 1)

                def turn(b, h):
                    pe.wait_ge(scaled, b * HEADS + h + 1)
                    if h >= 1:
                        pe.wait_ge(probT_ready, b * HEADS + h)
                    for kt in range(2):
                        for qt in range(2):
                            last = nc.tensor.transpose(turn_ps[:, kt * SEQ + qt * P:kt * SEQ + (qt + 1) * P],
                                                       prob[:, h % 8, qt, kt * P:(kt + 1) * P], ident[:, :])
                    last.then_inc(prob_turned, 1)

                def context(b, p):
                    pe.wait_ge(probT_ready, b * HEADS + 2 * p + 2)
                    if p >= 1:
                        pe.wait_ge(ctxT_ready, b * PAIRS + p)
                    for kt in range(2):
                        for hh in range(2):
                            r, h = DH * hh, 2 * p + hh
                            last = nc.tensor.matmul(ctx_ps[r:r + DH, 0:SEQ], v_s[:, kt, h * DH:(h + 1) * DH],
                                                    probT[:, h % 4, kt, :], start=(kt == 0), stop=(kt == 1))
                    last.then_inc(context_done, 1)

                def project(b, s):
                    here = out_ps[:, s * D:(s + 1) * D]
                    for p in range(PAIRS):
                        nc.tensor.matmul(here, ctxT[:, p, s * P:(s + 1) * P], wo_s[:, p, :], start=(p == 0), stop=False)
                    nc.tensor.matmul(here, ones_row[:, :], bias_row[:, :], start=False, stop=True).then_inc(out_done, 1)

                pe.wait_ge(weights_in, 16 * 5)
                pe.wait_ge(q_scaled, 2)
                turn_xn(0, True)
                for u in range(NU):
                    unit(0, u)
                turn_xn(1, False)
                scores(0, 0, True)
                scores(0, 1, True)
                with pe.Fori(0, BATCH) as b:
                    for t in range(PAIRS):
                        turn(b, 2 * t)
                        n, h = later(b, 2 * t + AHEAD)
                        scores(n, h // 2)
                        turn(b, 2 * t + 1)
                        unit(b + 1, UNITS.index(("qk", t)))
                        if t >= 1:
                            context(b, t - 1)
                        if t in (5, 6):
                            unit(b + 1, UNITS.index(("v", (t - 5, 0))))
                    unit(b + 1, NU - 2)
                    context(b, PAIRS - 1)
                    pe.wait_ge(ctxT_ready, b * PAIRS + PAIRS)
                    project(b, 0)
                    unit(b + 1, NU - 1)
                    project(b, 1)
                    turn_xn(b + 2, False)

            @block.scalar
            def _(act):
                def take_qk(n, p, first):
                    act.wait_ge(unit_done, n * NU + UNITS.index(("qk", p)) + 1)
                    if not first:
                        act.wait_ge(scores_done, n * PAIRS + p + 1 - PAIRS)
                    nc.scalar.activation(qkT[:, p, :, :].rearrange("p a q -> p (a q)"), unit_ps[:, :], ACT.Copy).then_inc(unit_taken, 1)

                def take_v(n, u, first):
                    s, half = UNITS[u][1]
                    act.wait_ge(unit_done, n * NU + u + 1)
                    if not first:
                        act.wait_ge(context_done, n * PAIRS - PAIRS + 4 * (half + 1))
                    nc.scalar.activation(v_s[:, s, half * 512:(half + 1) * 512], unit_ps[:, :], ACT.Copy).then_inc(unit_taken, 1)

                def exps(n, h, first=False):
                    act.wait_ge(max_done, n * HEADS + h + 1)
                    if not first:
                        act.wait_ge(prob_turned, n * HEADS + h - 7)
                    for qt in range(2):
                        last = nc.scalar.activation(prob[:, h % 8, qt, :], score_ps(h)[:, qt * SEQ:(qt + 1) * SEQ], ACT.Exp,
                                                    bias=neg_max[:, h, qt:qt + 1], accum_out=row_sum[:, h, qt:qt + 1])
                    last.then_inc(exp_done, 1)

                def take_turned(b, h):
                    act.wait_ge(prob_turned, b * HEADS + h + 1)
                    if h >= 4:
                        act.wait_ge(context_done, b * PAIRS + (h - 4) // 2 + 1)
                    nc.scalar.activation(probT[:, h % 4, :, :].rearrange("p k q -> p (k q)"), turn_ps[:, :],
                                         ACT.Copy).then_inc(probT_ready, 1)

                for u, (what, w) in enumerate(UNITS):
                    if what == "v":
                        take_v(0, u, True)
                    else:
                        take_qk(0, w, True)
                for h in range(EXP_AHEAD):
                    exps(0, h, True)

                def body(b, first):
                    for h in range(HEADS):
                        t = h // 2
                        take_turned(b, h)
                        if h % 2:
                            take_qk(b + 1, t, False)
                        exps(*later(b, h + EXP_AHEAD), first=first and h + EXP_AHEAD < 8)
                        if h % 2:
                            if t in (5, 6):
                                take_v(b + 1, UNITS.index(("v", (t - 5, 0))), False)
                    take_v(b + 1, NU - 2, False)
                    take_v(b + 1, NU - 1, False)
                body(0, True)
                with act.Fori(1, BATCH) as b:
                    body(b, False)

            @block.vector
            def _(dve):
                CHAIN = 2

                def row(n, s):
                    return xs[:, bass.ds(2 * n + s, 1), :].rearrange("p a d -> p (a d)")

                def normalise(n, part):
                    if part == 0:
                        for s in range(2):
                            last = nc.vector.bn_stats(stats[:, s, :], row(n, s))
                        last.then_inc(chain, 1)
                        dve.wait_ge(chain, n * CHAIN + 1)
                        nc.vector.memset(spare[:, :], 0.0)
                        for s in range(2):
                            last = nc.vector.bn_aggr(mean_var[:, s, :], stats[:, s, :])
                        last.then_inc(chain, 1)
                        dve.wait_ge(chain, n * CHAIN + 2)
                        nc.vector.tensor_scalar(var_eps[:, 0:2], mean_var[:, 0:2, 1], LN_EPS, None, ALU.add).then_inc(var_ready, 1)
                    else:
                        dve.wait_ge(rstd_ready, n + 1)
                        for s in range(2):
                            last = nc.vector.tensor_scalar(a_rows[:, s, :], row(n, s), mean_var[:, s, 0:1], rstd[:, s:s + 1],
                                                           ALU.subtract, ALU.mult)
                        last.then_inc(xn_ready, 1)

                def take_xn(n):
                    dve.wait_ge(xn_turned, n + 1)
                    nc.vector.tensor_copy(a_xnT[:, :], unit_ps[:, 0:SEQ]).then_inc(xnT_ready, 1)

                def maxes(n, h):
                    dve.wait_ge(scores_done, n * PAIRS + h // 2 + 1)
                    nc.vector.tensor_reduce(neg_max[:, h, :], score_ps(h)[:, :].rearrange("p (t k) -> p t k", k=SEQ),
                                            AX.X, ALU.max, negate=True).then_inc(max_done, 1)

                def scale(n, h):
                    dve.wait_ge(exp_done, n * HEADS + h + 1)
                    nc.vector.tensor_scalar(row_inv[:, h, :], row_sum[:, h, :], SOFTMAX_EPS, None, ALU.add).then_inc(sum_ready, 1)
                    dve.wait_ge(sum_ready, n * HEADS + h + 1)
                    nc.vector.reciprocal(row_inv[:, h, :], row_inv[:, h, :]).then_inc(inv_ready, 1)
                    dve.wait_ge(inv_ready, n * HEADS + h + 1)
                    for qt in range(2):
                        last = nc.vector.tensor_scalar(prob[:, h % 8, qt, :], prob[:, h % 8, qt, :], row_inv[:, h, qt:qt + 1],
                                                       None, ALU.mult)
                    last.then_inc(scaled, 1)

                def take_context(b, p):
                    dve.wait_ge(context_done, b * PAIRS + p + 1)
                    nc.vector.tensor_copy(ctxT[:, p, :], ctx_ps[:, 0:SEQ]).then_inc(ctxT_ready, 1)

                normalise(0, 0)
                normalise(0, 1)
                take_xn(0)
                normalise(1, 0)
                normalise(1, 1)
                take_xn(1)
                for h in range(AHEAD):
                    maxes(0, h)
                for h in range(SCALED_AHEAD):
                    scale(0, h)
                with dve.Fori(0, BATCH) as b:
                    for h in range(HEADS):
                        t = h // 2
                        if h % 2 == 0 and t >= 2:
                            take_context(b, t - 2)
                        maxes(*later(b, h + AHEAD))
                        scale(*later(b, h + SCALED_AHEAD))
                        if h == 3:
                            normalise(b + 2, 0)
                        if h == 7:
                            normalise(b + 2, 1)
                    take_context(b, PAIRS - 2)
                    take_context(b, PAIRS - 1)
                    dve.wait_ge(out_done, 2 * b + 2)
                    here = xs[:, bass.ds(2 * b, 2), :]
                    nc.vector.tensor_tensor(here, here, out_ps[:, 0:2 * D].rearrange("p (s d) -> p s d", d=D),
                                            ALU.add).then_inc(added, 1)
                    take_xn(b + 2)

        with nc.Block() as block:
            feed_forward(block, 0, [(gate_proj, gate_hi, gate_lo), (up_proj, up_hi, up_lo), (down_proj, down_hi, down_lo)])
        with nc.Block() as block:
            attention(block)
        with nc.Block() as block:
            feed_forward(block, 1, [(down_proj, down_hi, down_lo)])


_SHAPE = (16, 256, 128)


def kernel(**inputs):
    import numpy as _np
    import concourse.bacc as _bacc
    from concourse import mybir as _mybir
    from concourse.bass_utils import run_bass_kernel_spmd as _run

    a = {k[3:]: _np.asarray(v) for k, v in inputs.items()}
    def columns(w):
        w = w.reshape(GROUPS, GE, D, CPG, FS).transpose(2, 0, 3, 1, 4)
        return w.reshape(D, GROUPS, GW)
    down = a["ffn_down_proj"].reshape(GROUPS, GE, CPG, FS, D).transpose(1, 3, 0, 2, 4).reshape(P, GROUPS, GW)
    laid = {
        "x": a["attn_x"],
        "wq": a["attn_Wq"].T, "wk": a["attn_Wk"].T, "wv": a["attn_Wv"].T,
        "wo": a["attn_Wo"].T.reshape(PAIRS, P, D).transpose(1, 0, 2),
        "bo": a["attn_bo"].reshape(1, D),
        "gate_w": a["ffn_gate_w"].T,
        "gate_proj": columns(a["ffn_gate_proj"]), "up_proj": columns(a["ffn_up_proj"]), "down_proj": down,
    }
    nc = _bacc.Bacc("TRN2", target_bir_lowering=False, num_devices=1)
    arrays, args = {}, {}
    for name, v in laid.items():
        arrays[f"in_{name}"] = v = _np.ascontiguousarray(v)
        args[name] = nc.dram_tensor(f"in_{name}", v.shape, _mybir.dt.from_np(v.dtype), kind="ExternalInput").ap()
    args["out"] = nc.dram_tensor("out_x", _SHAPE, _mybir.dt.float32, kind="ExternalOutput").ap()
    macaron_block(nc, **args)
    r = _run(nc, [arrays], core_ids=[0])
    return r.results[0]["out_x"]
```

```python
import concourse.bass as bass
from concourse import mybir
from contextlib import ExitStack

FP32 = mybir.dt.float32
FP32R = mybir.dt.float32r
ALU = mybir.AluOpType
ACT = mybir.ActivationFunctionType
AX = mybir.AxisListType

P = 128
D = 128
BATCH, SEQ = 16, 256
E, F, TOP_K = 64, 96, 8
HEADS, DH = 16, 64
INNER = HEADS * DH
LN_EPS, SOFTMAX_EPS = 1e-5, 1e-10

TILES = BATCH * SEQ // P
BT = 4
NB = BT * P
BLOCKS = TILES // BT
GE = 4
GROUPS = E // GE
FS = P // GE
CPG = F // FS
CHUNKS = GROUPS * CPG
GW = CPG * P
UNROLL = 2
GPL = 2
LAG = 3
PAIR_CHUNKS = UNROLL * CHUNKS

STATS_AT, NORM_AT, TURN_AT, SPLIT_AT, LOGIT_AT, SHIFT_AT = 3, 6, 9, 12, 15, 18
EXP_AT, PROB_AT, TOP_AT, PICK_AT, WEIGHT_AT, WTURN_AT, WCOPY_AT = 20, 24, 27, 30, 33, 36, 39

PAIRS = HEADS // 2
PROB_SLOTS = 4


def macaron_block(nc, x, wq, wk, wv, wo, bo, gate_w, gate_proj, up_proj, down_proj, out):
    x_v = x.rearrange("b (p s) d -> p b (s d)", s=2)
    out_v = out.rearrange("b (p s) d -> p b (s d)", s=2)

    ctx = ExitStack()
    with ctx:
        def sb(name, shape, dt=FP32, scope=ctx):
            return scope.enter_context(nc.sbuf_tensor(name, shape, dt))

        def sem(name):
            return ctx.enter_context(nc.semaphore(name))

        def weight_parts(name, scope=ctx):
            hi = sb(f"{name}_hi", [P, GROUPS, GW], FP32R, scope)
            with nc.sbuf_tensor(f"{name}_raw", [P, GROUPS, GW], FP32) as raw:
                pass
            return raw, hi, sb(f"{name}_lo", [P, GROUPS, GW], FP32R, scope)

        gate_raw, gate_hi, gate_lo = weight_parts("gate")
        up_raw, up_hi, up_lo = weight_parts("up")
        xs = sb("xs", [P, TILES + BT, D])
        ident = sb("ident", [P, P])
        rw = sb("rw", [P, E])
        rw_hi = sb("rw_hi", [P, E], FP32R)
        rw_lo = sb("rw_lo", [P, E], FP32R)
        stats = sb("stats", [P, BT, 6])
        mean_var = sb("mean_var", [P, BT, 2])
        var_eps = sb("var_eps", [P, BT])
        rstd = sb("rstd", [P, BT])
        neg_half = sb("neg_half", [P, BT])
        spare = sb("spare", [P, 1])

        with ExitStack() as ffn_scope:
            def fb(name, shape, dt=FP32):
                return sb(name, shape, dt, ffn_scope)
            down_raw, down_hi, down_lo = weight_parts("down", ffn_scope)
            spread = fb("spread", [P, GROUPS, P], FP32R)
            act_buf = fb("act_buf", [P, 3, NB])
            h_hi = fb("h_hi", [P, LAG, NB], FP32R)
            h_lo = fb("h_lo", [P, LAG, NB], FP32R)
            xnT_hi = fb("xnT_hi", [P, 2, NB], FP32R)
            xnT_lo = fb("xnT_lo", [P, 2, NB], FP32R)
            wT = fb("wT", [P, 2, NB], FP32R)
            rows = fb("rows", [P, BT, D])
            yT = rows[:, :, :].rearrange("p t d -> p (t d)")
            probs = fb("probs", [P, BT, E])
            rest = fb("rest", [P, BT, E])
            best = fb("best", [P, BT, TOP_K])
            col = fb("col", [P, 6, BT])

        with ExitStack() as attn_scope:
            def ab(name, shape, dt=FP32):
                return sb(name, shape, dt, attn_scope)
            w_hi = ab("w_hi", [P, 3, INNER], FP32R)
            w_lo = ab("w_lo", [P, 3, INNER], FP32R)
            wo_s = ab("wo_s", [P, PAIRS, D])
            bias = ab("bias", [P, D])
            qk_hi = ab("qk_hi", [P, PAIRS, 2, SEQ], FP32R)
            qk_lo = ab("qk_lo", [P, PAIRS, 2, SEQ], FP32R)
            v_s = ab("v_s", [P, 2, INNER])
            prob = ab("prob", [P, PROB_SLOTS, 2, SEQ])
            probT = ab("probT", [P, 4, 2, SEQ])
            ctxT = ab("ctxT", [P, 2, SEQ])
            a_rows = ab("a_rows", [P, 2, D])
            a_xnT_hi = ab("a_xnT_hi", [P, SEQ], FP32R)
            a_xnT_lo = ab("a_xnT_lo", [P, SEQ], FP32R)
            unused = ab("unused", [P, 1])
            neg_max = ab("neg_max", [P, HEADS, 2])
            row_sum = ab("row_sum", [P, HEADS, 2])
            row_inv = ab("row_inv", [P, HEADS, 2])

        bank = [ctx.enter_context(nc.psum_tensor(f"bank{i}", [P, 512], FP32)) for i in range(8)]

        consts = sem("consts")
        first_x_in = sem("first_x_in")
        x_in = sem("x_in")
        x_out = sem("x_out")
        small_in = sem("small_in")
        rw_split = sem("rw_split")

        def feed_forward(block, ph, loads):
            def s(name):
                return sem(f"{name}{ph}")
            NW = len(loads)
            WAYS = [[s(f"weight_in{g}_{m}_") for m in range(NW)] for g in range(GROUPS // GPL)]
            weight_hi, weight_lo = s("weight_hi"), s("weight_lo")
            chain = s("chain")
            var_ready, rstd_ready, xn_ready = s("var_ready"), s("rstd_ready"), s("xn_ready")
            xn_turned, xnT_ready = s("xn_turned"), s("xnT_ready")
            logits_done, shifted, exp_done = s("logits_done"), s("shifted"), s("exp_done")
            weights_ready, weights_turned, wT_ready = s("weights_ready"), s("weights_turned"), s("wT_ready")
            spread_made, spread_done, gate_done, up_done = s("spread_made"), s("spread_done"), s("gate_done"), s("up_done")
            silu_done, scaled, h_done = s("silu_done"), s("scaled"), s("h_done")
            hi_done, lo_done, down_done = s("hi_done"), s("lo_done"), s("down_done")
            yT_done, y_turned, x_added = s("yT_done"), s("y_turned"), s("x_added")

            gate_ps, up_ps, w_ps = bank[0:2], bank[2:5], bank[5]
            y_ps, aux = bank[6], bank[7]
            SPLITS = [(g, m) for g in range(GROUPS) for m in range(NW)]
            EARLY = 2 * NW

            def splits_at(c):
                return [n for n in range(EARLY, len(SPLITS)) if (n - EARLY) * CPG // NW == c]

            def split_count(g, m):
                return SPLITS.index((g, m)) + 1

            def over_pairs(engine, body):
                body(0, True)
                with engine.Fori(1, BLOCKS // UNROLL) as i:
                    body(i, False)

            def positions():
                for c in range(PAIR_CHUNKS):
                    yield c, c // CHUNKS, c % CHUNKS

            def block_before(first, blk, k):
                return k == LAG and not (first and blk == 0)

            @block.sync
            def _(sp):
                if ph == 0:
                    sp.dma_start(xs[:, 0:BT, :].rearrange("p (b s) d -> p b (s d)", s=2), x_v[:, 0:2, :]).then_inc(first_x_in, 16)
                for g in range(GROUPS // GPL):
                    for m, (view, raw, _hi, _lo) in enumerate(loads):
                        some = slice(g * GPL, (g + 1) * GPL)
                        sp.dma_start(raw[:, some, :], view[:, some, :]).then_inc(WAYS[g][m], 16)
                    if ph == 0 and g == 0:
                        sp.dma_start(xs[:, BT:TILES, :].rearrange("p (b s) d -> p b (s d)", s=2), x_v[:, 2:BATCH, :]).then_inc(x_in, 16)
                if ph == 1:
                    with sp.Fori(0, BLOCKS) as i:
                        sp.wait_ge(x_added, i + 1)
                        sp.dma_start(out_v[:, bass.ds(2 * i, 2), :],
                                     xs[:, bass.ds(BT * i, BT), :].rearrange("p (b s) d -> p b (s d)", s=2)).then_inc(x_out, 16)
                    sp.wait_ge(x_out, 16 * BLOCKS)

            @block.gpsimd
            def _(pool):
                if ph == 0:
                    nc.gpsimd.memset(neg_half[:, :], -0.5).then_inc(consts, 1)
                    nc.gpsimd.memset(ident[:, :], 0.0).then_inc(consts, 1)
                    nc.gpsimd.memset(xs[:, TILES:TILES + BT, :], 0.0).then_inc(consts, 1)
                    pool.wait_ge(consts, 3)
                    nc.gpsimd.affine_select(out=ident[:, :], in_=ident[:, :], compare_op=ALU.not_equal, fill=1.0,
                                            base=0, pattern=[[-1, P]], channel_multiplier=1).then_inc(consts, 1)
                def rstd_of(count):
                    pool.wait_ge(var_ready, count)
                    nc.gpsimd.tensor_tensor(rstd[:, :], var_eps[:, :], neg_half[:, :], ALU.pow).then_inc(rstd_ready, 1)

                rstd_of(1)
                nc.gpsimd.memset(spread[:, :, :].bitcast(FP32), 0.0).then_inc(spread_made, 1)
                wide = spread[:, :, :].rearrange("p g (i k) -> p (g i) k", k=FS)
                for n in range(2):
                    pool.wait_ge(spread_made, n + 1)
                    nc.gpsimd.affine_select(out=wide, in_=wide.bitcast(FP32), compare_op=ALU.not_equal, fill=1.0,
                                            base=-E * n, pattern=[[-1, E], [0, FS]], channel_multiplier=1).then_inc(spread_made, 1)

                def body(i, first):
                    for c, blk, k in positions():
                        if k == STATS_AT:
                            rstd_of(i * UNROLL + blk + 2)
                        pool.wait_ge(hi_done, i * PAIR_CHUNKS + c + 1)
                        if not first or c >= LAG:
                            pool.wait_ge(down_done, i * PAIR_CHUNKS + c - LAG + 1)
                        nc.gpsimd.tensor_tensor(h_lo[:, c % LAG, :], act_buf[:, c % 3, :], h_hi[:, c % LAG, :].bitcast(FP32),
                                                ALU.subtract).then_inc(lo_done, 1)
                over_pairs(pool, body)

            @block.scalar
            def _(act):
                if ph == 0:
                    act.dma_start(rw[:, :], gate_w).then_inc(small_in, 16)

                def high_part(n):
                    g, m = SPLITS[n]
                    _view, raw, hi, _lo = loads[m]
                    act.wait_ge(WAYS[g // GPL][m], 16)
                    nc.scalar.activation(hi[:, g, :], raw[:, g, :], ACT.Copy).then_inc(weight_hi, 1)

                def exp_of(count):
                    act.wait_ge(shifted, count)
                    nc.scalar.activation(probs[:, :, :], rest[:, :, :], ACT.Exp).then_inc(exp_done, 1)

                def take_yT(down):
                    act.wait_ge(down_done, down)
                    nc.scalar.activation(yT[:, :], y_ps[:, :], ACT.Copy).then_inc(yT_done, 1)

                for n in range(EARLY):
                    high_part(n)
                exp_of(1)

                def high_h(i, c, reused):
                    act.wait_ge(h_done, i * PAIR_CHUNKS + c + 1)
                    if reused:
                        act.wait_ge(down_done, i * PAIR_CHUNKS + c + 1 - LAG)
                    nc.scalar.activation(h_hi[:, c % LAG, :], act_buf[:, c % 3, :], ACT.Copy).then_inc(hi_done, 1)

                def body(i, first):
                    for c, blk, k in positions():
                        if block_before(first, blk, k):
                            take_yT(i * PAIR_CHUNKS + blk * CHUNKS)
                        act.wait_ge(gate_done, i * PAIR_CHUNKS + c + 1)
                        if not first or c >= 3:
                            act.wait_ge(lo_done, i * PAIR_CHUNKS + c - 2)
                        nc.scalar.activation(act_buf[:, c % 3, :], gate_ps[c % 2][:, :], ACT.Silu).then_inc(silu_done, 1)
                        if not first or c >= 1:
                            high_h(i, c - 1, not first or c - 1 >= LAG)
                        if first:
                            for n in splits_at(c):
                                high_part(n)
                        if k == EXP_AT:
                            exp_of(i * UNROLL + blk + 2)
                over_pairs(act, body)
                high_h(0, BLOCKS * CHUNKS - 1, True)
                take_yT(BLOCKS * CHUNKS)

            @block.tensor
            def _(pe):
                def split_product(ps, hi, lo, m_hi, m_lo, start, stop):
                    nc.tensor.matmul(ps, hi, m_hi, start=start, stop=False)
                    nc.tensor.matmul(ps, hi, m_lo, start=False, stop=False)
                    return nc.tensor.matmul(ps, lo, m_hi, start=False, stop=stop)

                def turn_rows(ready, count, done):
                    pe.wait_ge(ready, count)
                    for t in range(BT):
                        last = nc.tensor.transpose(aux[:, t * P:(t + 1) * P], rows[:, t, :], ident[:, :])
                    last.then_inc(done, 1)

                def logits(count, slot):
                    pe.wait_ge(xnT_ready, count)
                    for t in range(BT):
                        a, b = t * P, (t + 1) * P
                        last = split_product(aux[:, t * E:(t + 1) * E], xnT_hi[:, slot, a:b], xnT_lo[:, slot, a:b],
                                             rw_hi[:, :], rw_lo[:, :], True, True)
                    last.then_inc(logits_done, 1)

                def turn_y(count, routings):
                    pe.wait_ge(yT_done, count)
                    pe.wait_ge(wT_ready, routings)
                    for t in range(BT):
                        last = nc.tensor.transpose(aux[:, t * P:(t + 1) * P], yT[:, t * P:(t + 1) * P], ident[:, :])
                    last.then_inc(y_turned, 1)

                pe.wait_ge(consts, 4)
                if ph == 0:
                    pe.wait_ge(rw_split, 2)
                turn_rows(xn_ready, 1, xn_turned)
                logits(1, 0)

                def split_weights(first, blk, g, m):
                    if first and blk == 0 and (g, m) in SPLITS:
                        pe.wait_ge(weight_lo, split_count(g, m))

                def gate_up(i, c, first):
                    blk, k = c // CHUNKS, c % CHUNKS
                    G, a, b = k // CPG, (k % CPG) * P, (k % CPG + 1) * P
                    if k == 0:
                        pe.wait_ge(xnT_ready, i * UNROLL + blk + 1)
                    if not first or c >= 2:
                        pe.wait_ge(silu_done, i * PAIR_CHUNKS + c - 1)
                    if k % CPG == 0 and NW == 3:
                        split_weights(first, blk, G, 1)
                    split_product(gate_ps[c % 2][:, :], gate_hi[:, G, a:b], gate_lo[:, G, a:b],
                                  xnT_hi[:, blk, :], xnT_lo[:, blk, :], True, True).then_inc(gate_done, 1)
                    if not first or c >= 3:
                        pe.wait_ge(h_done, i * PAIR_CHUNKS + c - 2)
                    split_product(up_ps[c % 3][:, :], up_hi[:, G, a:b], up_lo[:, G, a:b],
                                  xnT_hi[:, blk, :], xnT_lo[:, blk, :], True, True).then_inc(up_done, 1)

                def spread_weights(i, c, first):
                    blk, G = c // CHUNKS, c % CHUNKS // CPG
                    if G == 0:
                        pe.wait_ge(wT_ready, i * UNROLL + blk + 1)
                    if not first or c >= 1:
                        pe.wait_ge(scaled, i * PAIR_CHUNKS + c)
                    nc.tensor.matmul(w_ps[:, :], spread[:, G, :], wT[:, blk, :],
                                     start=True, stop=True).then_inc(spread_done, 1)

                def down(i, d, first, taken):
                    kd = d % CHUNKS
                    G, a, b = kd // CPG, (kd % CPG) * P, (kd % CPG + 1) * P
                    pe.wait_ge(lo_done, i * PAIR_CHUNKS + d + 1)
                    if kd % CPG == 0:
                        split_weights(first, d // CHUNKS, G, NW - 1)
                    if taken is not None:
                        pe.wait_ge(yT_done, taken)
                    split_product(y_ps[:, :], down_hi[:, G, a:b], down_lo[:, G, a:b],
                                  h_hi[:, d % LAG, :], h_lo[:, d % LAG, :], kd == 0, kd == CHUNKS - 1).then_inc(down_done, 1)

                def body(i, first):
                    for c, blk, k in positions():
                        if first and c == 0:
                            for ahead in range(LAG):
                                gate_up(i, ahead, first)
                            turn_rows(weights_ready, 2, weights_turned)
                            pe.wait_ge(spread_made, 3)
                        if not first or c >= LAG:
                            gate_up(i, c, first)
                        if k % CPG == 0:
                            spread_weights(i, c, first)
                        before = i * UNROLL + blk
                        if not first or c >= LAG:
                            down(i, c - LAG, first, before if block_before(first, blk, k) else None)
                        if block_before(first, blk, k):
                            turn_y(before, before + 1)
                        nxt = before + 2
                        if k == TURN_AT:
                            turn_rows(xn_ready, nxt, xn_turned)
                        if k == LOGIT_AT:
                            logits(nxt, 1 - blk)
                        if k == WTURN_AT:
                            turn_rows(weights_ready, 2 * nxt, weights_turned)
                over_pairs(pe, body)
                for d in range(BLOCKS * CHUNKS - LAG, BLOCKS * CHUNKS):
                    down(0, d, False, None)
                turn_y(BLOCKS, BLOCKS + 1)

            @block.vector
            def _(dve):
                if ph == 0:
                    dve.wait_ge(small_in, 16)
                    nc.vector.tensor_copy(rw_hi[:, :], rw[:, :]).then_inc(rw_split, 1)
                    dve.wait_ge(rw_split, 1)
                    nc.vector.tensor_tensor(rw_lo[:, :], rw[:, :], rw_hi[:, :].bitcast(FP32), ALU.subtract).then_inc(rw_split, 1)
                    dve.wait_ge(first_x_in, 16)
                    dve.wait_ge(consts, 4)

                CHAIN = 2 + 5 + 7
                def over_experts(a):
                    return a.unsqueeze(2).broadcast_to([P, BT, E])

                def stage(k, tile0, done, nth, slot):
                    def step(ins, n):
                        ins.then_inc(chain, 1)
                        dve.wait_ge(chain, done + n)
                    if k == STATS_AT:
                        for t in range(BT):
                            last = nc.vector.bn_stats(stats[:, t, :], xs[:, bass.ds(tile0 + t, 1), :].rearrange("p a d -> p (a d)"))
                        step(last, 1)
                        nc.vector.memset(spare[:, :], 0.0)
                        for t in range(BT):
                            last = nc.vector.bn_aggr(mean_var[:, t, :], stats[:, t, :])
                        step(last, 2)
                        nc.vector.tensor_scalar(var_eps[:, :], mean_var[:, :, 1], LN_EPS, None, ALU.add).then_inc(var_ready, 1)
                    if k == NORM_AT:
                        dve.wait_ge(rstd_ready, nth)
                        for t in range(BT):
                            last = nc.vector.tensor_scalar(rows[:, t, :], xs[:, bass.ds(tile0 + t, 1), :].rearrange("p a d -> p (a d)"),
                                                           mean_var[:, t, 0:1], rstd[:, t:t + 1], ALU.subtract, ALU.mult)
                        last.then_inc(xn_ready, 1)
                    if k == SPLIT_AT:
                        dve.wait_ge(xn_turned, nth)
                        step(nc.vector.tensor_copy(xnT_hi[:, slot, :], aux[:, :]), 3)
                        nc.vector.tensor_tensor(xnT_lo[:, slot, :], aux[:, :], xnT_hi[:, slot, :].bitcast(FP32),
                                                ALU.subtract).then_inc(xnT_ready, 1)
                    lg = aux[:, 0:BT * E].rearrange("p (t e) -> p t e", e=E)
                    if k == SHIFT_AT:
                        dve.wait_ge(logits_done, nth)
                        step(nc.vector.tensor_reduce(col[:, 0, :], lg, AX.X, ALU.max), 4)
                        nc.vector.tensor_tensor(rest[:, :, :], lg, over_experts(col[:, 0, :]), ALU.subtract).then_inc(shifted, 1)
                    if k == PROB_AT:
                        dve.wait_ge(exp_done, nth)
                        step(nc.vector.tensor_reduce(col[:, 1, :], probs[:, :, :], AX.X, ALU.add), 5)
                        step(nc.vector.reciprocal(col[:, 2, :], col[:, 1, :]), 6)
                        nc.vector.tensor_tensor(probs[:, :, :], probs[:, :, :], over_experts(col[:, 2, :]), ALU.mult).then_inc(chain, 1)
                    if k == TOP_AT:
                        dve.wait_ge(chain, done + 7)
                        nc.vector.memset(spare[:, :], 0.0)
                        for t in range(BT):
                            last = nc.vector.max(best[:, t, :], probs[:, t, :])
                        last.then_inc(chain, 1)
                    if k == PICK_AT:
                        dve.wait_ge(chain, done + 8)
                        nc.vector.memset(spare[:, :], 0.0)
                        for t in range(BT):
                            last = nc.vector.match_replace(rest[:, t, :], best[:, t, :], probs[:, t, :], -1.0)
                        step(last, 9)
                        step(nc.vector.tensor_reduce(col[:, 3, :], best[:, :, :], AX.X, ALU.add), 10)
                        step(nc.vector.reciprocal(col[:, 4, :], col[:, 3, :]), 11)
                    if k == WEIGHT_AT:
                        step(nc.vector.tensor_scalar(col[:, 5, :], col[:, 4, :], -0.5, None, ALU.mult), 12)
                        step(nc.vector.scalar_tensor_tensor(out=rest[:, :, :], in0=rest[:, :, :], scalar=0.0, in1=probs[:, :, :],
                                                            op0=ALU.max, op1=ALU.subtract), 13)
                        nc.vector.tensor_tensor(probs[:, :, :], rest[:, :, :], over_experts(col[:, 5, :]), ALU.mult).then_inc(chain, 1)
                        dve.wait_ge(chain, done + CHAIN)
                        hi = rows[:, :, 0:E].bitcast(FP32R)
                        nc.vector.tensor_copy(hi, probs[:, :, :]).then_inc(weights_ready, 1)
                        dve.wait_ge(weights_ready, 2 * nth - 1)
                        nc.vector.tensor_tensor(rows[:, :, E:2 * E].bitcast(FP32R), probs[:, :, :], rows[:, :, 0:E],
                                                ALU.subtract).then_inc(weights_ready, 1)
                    if k == WCOPY_AT:
                        dve.wait_ge(weights_turned, nth)
                        nc.vector.tensor_copy(wT[:, slot, :], aux[:, :]).then_inc(wT_ready, 1)

                STAGES = (STATS_AT, NORM_AT, SPLIT_AT, SHIFT_AT, PROB_AT, TOP_AT, PICK_AT, WEIGHT_AT, WCOPY_AT)

                def add_y(count, tile0):
                    dve.wait_ge(y_turned, count)
                    here = xs[:, bass.ds(tile0, BT), :]
                    nc.vector.tensor_tensor(here, here, aux[:, :].rearrange("p (t d) -> p t d", d=D), ALU.add).then_inc(x_added, 1)

                def low_part(n):
                    g, m = SPLITS[n]
                    _view, raw, hi, lo = loads[m]
                    dve.wait_ge(weight_hi, n + 1)
                    nc.vector.tensor_tensor(lo[:, g, :], raw[:, g, :], hi[:, g, :].bitcast(FP32), ALU.subtract).then_inc(weight_lo, 1)

                for k in STAGES:
                    stage(k, 0, 0, 1, 0)
                    if k == NORM_AT and ph == 0:
                        for n in range(2):
                            low_part(n)
                    if k == SPLIT_AT:
                        for n in range(2 if ph == 0 else 0, EARLY):
                            low_part(n)
                if ph == 0:
                    dve.wait_ge(x_in, 16)

                def body(i, first):
                    for c, blk, k in positions():
                        at = i * PAIR_CHUNKS + c + 1
                        buf = act_buf[:, c % 3, :]
                        dve.wait_ge(silu_done, at)
                        if c % CPG == 0:
                            dve.wait_ge(spread_done, i * (PAIR_CHUNKS // CPG) + c // CPG + 1)
                        nc.vector.tensor_tensor(buf, buf, w_ps[:, :], ALU.mult).then_inc(scaled, 1)
                        dve.wait_ge(scaled, at)
                        dve.wait_ge(up_done, at)
                        nc.vector.tensor_tensor(buf, buf, up_ps[c % 3][:, :], ALU.mult).then_inc(h_done, 1)
                        if first:
                            for n in splits_at(c):
                                low_part(n)
                        before = i * UNROLL + blk
                        if k in STAGES:
                            stage(k, (before + 1) * BT, (before + 1) * CHAIN, before + 2, 1 - blk)
                        if block_before(first, blk, k):
                            add_y(before, (before - 1) * BT)
                over_pairs(dve, body)
                add_y(BLOCKS, (BLOCKS - 1) * BT)

        def attention(block):
            piece_in, wo_in, bias_in, bias_added = [sem(f"piece{n}_in") for n in range(5)], sem("wo_in"), sem("bias_in"), sem("bias_added")
            w_hi_done, w_lo_done, qk_hi_done, projected = sem("w_hi_done"), sem("w_lo_done"), sem("qk_hi_done"), sem("projected")
            chain, var_ready, rstd_ready, xn_ready = sem("a_chain"), sem("a_var_ready"), sem("a_rstd_ready"), sem("a_xn_ready")
            xn_turned, xnT_hi_done, xnT_ready, unit_done = sem("a_xn_turned"), sem("a_xnT_hi_done"), sem("a_xnT_ready"), sem("unit_done")
            unit_taken = sem("unit_taken")
            scores_done, max_done, exp_done, sum_ready, inv_ready, scaled = (
                sem("scores_done"), sem("max_done"), sem("a_exp_done"), sem("sum_ready"), sem("inv_ready"), sem("a_scaled"))
            prob_turned, probT_ready, context_done, ctxT_ready = (sem("prob_turned"), sem("probT_ready"),
                                                                  sem("context_done"), sem("ctxT_ready"))
            added = sem("a_added")

            turn_ps, unit_ps, ctx_ps, out_ps = bank[4:8]
            UNITS = [("qk", 0), ("qk", 1), ("qk", 2), ("v", (0, 0)), ("qk", 3), ("qk", 4), ("v", (1, 0)), ("qk", 5),
                     ("v", (0, 1)), ("qk", 6), ("v", (1, 1)), ("qk", 7)]
            NU = len(UNITS)
            LATE = 8
            EVEN, ODD = range(2)
            UNIT_AT = {(2, ODD): 0, (3, ODD): 1, (4, ODD): 2, (5, EVEN): 3, (5, ODD): 4, (6, ODD): 5, (7, EVEN): 6, (7, ODD): 7,
                       (0, EVEN): 8, (0, ODD): 9, (1, EVEN): 10, (1, ODD): 11}
            AHEAD = 4
            EXP_AHEAD = 3
            SCALED_AHEAD = 2

            w_staged = [prob[:, 0:2, :, :].rearrange("p a b c -> p (a b c)"), prob[:, 2:4, :, :].rearrange("p a b c -> p (a b c)"),
                        probT[:, 0:2, :, :].rearrange("p a b c -> p (a b c)")]
            W_SCALE = [DH ** -0.5, 1.0, 1.0]
            NEAR, FAR, ALL = slice(0, INNER // 2), slice(INNER // 2, INNER), slice(0, INNER)
            W_PIECES = [(0, NEAR), (1, NEAR), (2, ALL), (0, FAR), (1, FAR)]
            NEAR_QK, NEAR_QKV, ALL_QKV = 2, 3, 5

            def unit_bank(u, first):
                return turn_ps if first and u % 2 else unit_ps

            def score_ps(h):
                return bank[h % 4]

            def first_batch(n):
                return isinstance(n, int) and n == 0

            def exists(n):
                return not isinstance(n, int) or n < BATCH

            def unit_at(n, t, place):
                if (t, place) not in UNIT_AT:
                    return []
                u = UNIT_AT[t, place]
                made_for = n if u >= LATE else n + 1
                return [(made_for, u)] if exists(made_for) else []

            def all_steps(engine, step):
                def body(b):
                    for t in range(2, PAIRS):
                        step(b, t, None)
                    for t in range(2):
                        step(b + 1, t, b)
                for t in range(2):
                    step(0, t, None)
                with engine.Fori(0, BATCH - 1) as b:
                    body(b)
                body(BATCH - 1)

            def later(b, h):
                return (b, h) if h < HEADS else (b + 1, h - HEADS)

            @block.sync
            def _(sp):
                for (m, cols), arrived in zip(W_PIECES, piece_in):
                    sp.dma_start(w_staged[m][:, cols], (wq, wk, wv)[m][:, cols]).then_inc(arrived, 16)
                sp.dma_start(wo_s[:, :, :], wo).then_inc(wo_in, 16)
                sp.dma_start(bias[:, :], bo.broadcast_to([P, D])).then_inc(bias_in, 16)

            @block.gpsimd
            def _(pool):
                def rstd_of(n):
                    pool.wait_ge(var_ready, n + 1)
                    nc.gpsimd.tensor_tensor(rstd[:, 0:2], var_eps[:, 0:2], neg_half[:, 0:2], ALU.pow).then_inc(rstd_ready, 1)

                def add_bias(n):
                    pool.wait_ge(xn_ready, n + 1)
                    here = xs[:, bass.ds(2 * n, 2), :]
                    nc.gpsimd.tensor_tensor(here, here, bias[:, :].unsqueeze(1).broadcast_to([P, 2, D]), ALU.add).then_inc(bias_added, 1)

                rstd_of(0)
                rstd_of(1)
                pool.wait_ge(bias_in, 16)
                add_bias(0)
                with pool.Fori(0, BATCH - 1) as b:
                    rstd_of(b + 2)
                    add_bias(b + 1)

            @block.tensor
            def _(pe):
                def turn_xn(n, first):
                    pe.wait_ge(xn_ready, n + 1)
                    if not first:
                        pe.wait_ge(unit_taken, n * NU)
                    for s in range(2):
                        last = nc.tensor.transpose(unit_ps[:, s * P:(s + 1) * P], a_rows[:, s, :], ident[:, :])
                    last.then_inc(xn_turned, 1)

                def unit(n, u, first=False):
                    what, w = UNITS[u]
                    unit_ps = unit_bank(u, first)
                    if u == 0:
                        pe.wait_ge(xnT_ready, n + 1)
                    elif first:
                        if u >= 2:
                            pe.wait_ge(unit_taken, u - 1)
                    else:
                        pe.wait_ge(unit_taken, n * NU + u)
                    if what == "v":
                        s, half = w
                        if first:
                            pe.wait_ge(w_lo_done, NEAR_QKV)
                        a, b = slice(s * P, (s + 1) * P), slice(half * 512, (half + 1) * 512)
                        for n_part, (m_x, m_w) in enumerate(((a_xnT_hi, w_hi), (a_xnT_hi, w_lo), (a_xnT_lo, w_hi))):
                            last = nc.tensor.matmul(unit_ps[:, :], m_x[:, a], m_w[:, 2, b], start=(n_part == 0), stop=(n_part == 2))
                    else:
                        if first and w >= PAIRS // 2:
                            pe.wait_ge(w_lo_done, ALL_QKV)
                        a = slice(w * P, (w + 1) * P)
                        for m in range(2):
                            for n_part, (m_w, m_x) in enumerate(((w_hi, a_xnT_hi), (w_hi, a_xnT_lo), (w_lo, a_xnT_hi))):
                                last = nc.tensor.matmul(unit_ps[:, m * SEQ:(m + 1) * SEQ], m_w[:, m, a], m_x[:, :],
                                                        start=(n_part == 0), stop=(n_part == 2))
                    last.then_inc(unit_done, 1)

                def scores(n, p):
                    pe.wait_ge(unit_taken, n * NU + UNITS.index(("qk", p)) + 1)
                    if p >= 2 or not first_batch(n):
                        pe.wait_ge(exp_done, n * HEADS + 2 * p - 2)
                    for qt in range(2):
                        for n_part, (m_q, m_k) in enumerate(((qk_hi, qk_hi), (qk_hi, qk_lo), (qk_lo, qk_hi))):
                            for hh in range(2):
                                r = slice(DH * hh, DH * hh + DH)
                                last = nc.tensor.matmul(score_ps(2 * p + hh)[:, qt * SEQ:(qt + 1) * SEQ],
                                                        m_q[r, p, 0, qt * P:(qt + 1) * P], m_k[r, p, 1, :],
                                                        start=(n_part == 0), stop=(n_part == 2))
                    last.then_inc(scores_done, 1)

                def turn(b, h):
                    pe.wait_ge(scaled, b * HEADS + h + 1)
                    if h >= 1 or not first_batch(b):
                        pe.wait_ge(probT_ready, b * HEADS + h)
                    for kt in range(2):
                        for qt in range(2):
                            last = nc.tensor.transpose(turn_ps[:, kt * SEQ + qt * P:kt * SEQ + (qt + 1) * P],
                                                       prob[:, h % PROB_SLOTS, qt, kt * P:(kt + 1) * P], ident[:, :])
                    last.then_inc(prob_turned, 1)

                def context(b, p):
                    pe.wait_ge(probT_ready, b * HEADS + 2 * p + 2)
                    if p >= 1 or not first_batch(b):
                        pe.wait_ge(ctxT_ready, b * PAIRS + p)
                    for kt in range(2):
                        for hh in range(2):
                            r, h = DH * hh, 2 * p + hh
                            last = nc.tensor.matmul(ctx_ps[r:r + DH, 0:SEQ], v_s[:, kt, h * DH:(h + 1) * DH],
                                                    probT[:, h % 4, kt, :], start=(kt == 0), stop=(kt == 1))
                    last.then_inc(context_done, 1)

                def project(b, p):
                    pe.wait_ge(ctxT_ready, b * PAIRS + p + 1)
                    for s in range(2):
                        last = nc.tensor.matmul(out_ps[:, s * D:(s + 1) * D], ctxT[:, p % 2, s * P:(s + 1) * P], wo_s[:, p, :],
                                                start=(p == 0 and s == 0), stop=(p == PAIRS - 1 and s == 1))
                    last.then_inc(projected, 1)

                turn_xn(0, True)
                pe.wait_ge(w_lo_done, NEAR_QK)
                for u in range(LATE):
                    unit(0, u, True)
                    if u in (1, 2):
                        scores(0, u - 1)
                pe.wait_ge(unit_taken, LATE)
                pe.wait_ge(wo_in, 16)

                def step(n, t, before):
                    if exists(n):
                        turn(n, 2 * t)
                    whose, pair = (n, t - 1) if t >= 1 else (before, PAIRS - 1)
                    made = whose is not None and exists(whose)
                    if made:
                        context(whose, pair)
                    if exists(n):
                        for unit_of in unit_at(n, t, EVEN):
                            unit(*unit_of)
                        if t == 2 and exists(n + 1):
                            turn_xn(n + 1, False)
                        m, h = later(n, 2 * t + AHEAD)
                        if exists(m):
                            scores(m, h // 2)
                        turn(n, 2 * t + 1)
                        for unit_of in unit_at(n, t, ODD):
                            unit(*unit_of)
                    if made:
                        project(whose, pair)
                all_steps(pe, step)

            @block.scalar
            def _(act):
                def take_unit(n, u, first=False):
                    what, w = UNITS[u]
                    act.wait_ge(unit_done, n * NU + u + 1)
                    if what == "qk":
                        nc.scalar.activation(qk_hi[:, w, :, :].rearrange("p a q -> p (a q)"), unit_bank(u, first)[:, :],
                                             ACT.Copy).then_inc(qk_hi_done, 1)
                    else:
                        s, half = w
                        if first:
                            act.wait_ge(unit_taken, u)
                        nc.scalar.activation(v_s[:, s, half * 512:(half + 1) * 512], unit_bank(u, first)[:, :],
                                             ACT.Copy).then_inc(unit_taken, 1)

                def exps(n, h):
                    act.wait_ge(max_done, n * HEADS + h + 1)
                    if h >= PROB_SLOTS or not first_batch(n):
                        act.wait_ge(prob_turned, n * HEADS + h + 1 - PROB_SLOTS)
                    for qt in range(2):
                        last = nc.scalar.activation(prob[:, h % PROB_SLOTS, qt, :], score_ps(h)[:, qt * SEQ:(qt + 1) * SEQ], ACT.Exp,
                                                    bias=neg_max[:, h, qt:qt + 1], accum_out=row_sum[:, h, qt:qt + 1])
                    last.then_inc(exp_done, 1)

                def take_turned(b, h):
                    act.wait_ge(prob_turned, b * HEADS + h + 1)
                    if h >= 4 or not first_batch(b):
                        act.wait_ge(context_done, b * PAIRS + (h - 4) // 2 + 1)
                    nc.scalar.activation(probT[:, h % 4, :, :].rearrange("p k q -> p (k q)"), turn_ps[:, :],
                                         ACT.Copy).then_inc(probT_ready, 1)

                def high_w(n):
                    m, cols = W_PIECES[n]
                    act.wait_ge(piece_in[n], 16)
                    nc.scalar.activation(w_hi[:, m, cols], w_staged[m][:, cols], ACT.Copy, scale=W_SCALE[m]).then_inc(w_hi_done, 1)

                nc.scalar.activation(unused[:, :], neg_half[:, 0:1], ACT.Exp)
                high_w(0)
                high_w(1)
                for u in range(LATE):
                    take_unit(0, u, True)
                    if u == 1:
                        high_w(2)
                        high_w(3)
                        high_w(4)
                    if u == 2:
                        act.wait_ge(w_lo_done, ALL_QKV)
                    if 2 <= u < 2 + EXP_AHEAD:
                        exps(0, u - 2)

                def step(n, t, before):
                    if not exists(n):
                        return
                    for place in (EVEN, ODD):
                        take_turned(n, 2 * t + place)
                        for unit_of in unit_at(n, t, place):
                            take_unit(*unit_of)
                        m, h = later(n, 2 * t + place + EXP_AHEAD)
                        if exists(m):
                            exps(m, h)
                all_steps(act, step)

            @block.vector
            def _(dve):
                CHAIN = 2

                def row(n, s):
                    return xs[:, bass.ds(2 * n + s, 1), :].rearrange("p a d -> p (a d)")

                def normalise(n, part):
                    if part == 0:
                        for s in range(2):
                            last = nc.vector.bn_stats(stats[:, s, :], row(n, s))
                        last.then_inc(chain, 1)
                        dve.wait_ge(chain, n * CHAIN + 1)
                        nc.vector.memset(spare[:, :], 0.0)
                        for s in range(2):
                            last = nc.vector.bn_aggr(mean_var[:, s, :], stats[:, s, :])
                        last.then_inc(chain, 1)
                        dve.wait_ge(chain, n * CHAIN + 2)
                        nc.vector.tensor_scalar(var_eps[:, 0:2], mean_var[:, 0:2, 1], LN_EPS, None, ALU.add).then_inc(var_ready, 1)
                    else:
                        dve.wait_ge(rstd_ready, n + 1)
                        for s in range(2):
                            last = nc.vector.tensor_scalar(a_rows[:, s, :], row(n, s), mean_var[:, s, 0:1], rstd[:, s:s + 1],
                                                           ALU.subtract, ALU.mult)
                        last.then_inc(xn_ready, 1)

                def take_xn(n):
                    dve.wait_ge(xn_turned, n + 1)
                    nc.vector.tensor_copy(a_xnT_hi[:, :], unit_ps[:, 0:SEQ]).then_inc(xnT_hi_done, 1)
                    dve.wait_ge(xnT_hi_done, n + 1)
                    nc.vector.tensor_tensor(a_xnT_lo[:, :], unit_ps[:, 0:SEQ], a_xnT_hi[:, :].bitcast(FP32),
                                            ALU.subtract).then_inc(xnT_ready, 1)

                def low_w(n):
                    m, cols = W_PIECES[n]
                    dve.wait_ge(w_hi_done, n + 1)
                    nc.vector.scalar_tensor_tensor(out=w_lo[:, m, cols], in0=w_staged[m][:, cols], scalar=W_SCALE[m],
                                                   in1=w_hi[:, m, cols].bitcast(FP32), op0=ALU.mult, op1=ALU.subtract).then_inc(w_lo_done, 1)

                def low_qk(n, p, first=False):
                    dve.wait_ge(qk_hi_done, n * PAIRS + p + 1)
                    nc.vector.tensor_tensor(qk_lo[:, p, :, :].rearrange("p a q -> p (a q)"),
                                            unit_bank(UNITS.index(("qk", p)), first)[:, :],
                                            qk_hi[:, p, :, :].rearrange("p a q -> p (a q)").bitcast(FP32),
                                            ALU.subtract).then_inc(unit_taken, 1)

                def maxes(n, h):
                    dve.wait_ge(scores_done, n * PAIRS + h // 2 + 1)
                    nc.vector.tensor_reduce(neg_max[:, h, :], score_ps(h)[:, :].rearrange("p (t k) -> p t k", k=SEQ),
                                            AX.X, ALU.max, negate=True).then_inc(max_done, 1)

                def scale(n, h):
                    dve.wait_ge(exp_done, n * HEADS + h + 1)
                    nc.vector.tensor_scalar(row_inv[:, h, :], row_sum[:, h, :], SOFTMAX_EPS, None, ALU.add).then_inc(sum_ready, 1)
                    dve.wait_ge(sum_ready, n * HEADS + h + 1)
                    nc.vector.reciprocal(row_inv[:, h, :], row_inv[:, h, :]).then_inc(inv_ready, 1)
                    dve.wait_ge(inv_ready, n * HEADS + h + 1)
                    for qt in range(2):
                        last = nc.vector.tensor_scalar(prob[:, h % PROB_SLOTS, qt, :], prob[:, h % PROB_SLOTS, qt, :], row_inv[:, h, qt:qt + 1],
                                                       None, ALU.mult)
                    last.then_inc(scaled, 1)

                def take_context(b, p):
                    dve.wait_ge(context_done, b * PAIRS + p + 1)
                    if p >= 2:
                        dve.wait_ge(projected, b * PAIRS + p - 1)
                    nc.vector.tensor_copy(ctxT[:, p % 2, :], ctx_ps[:, 0:SEQ]).then_inc(ctxT_ready, 1)

                normalise(0, 0)
                normalise(0, 1)
                take_xn(0)
                low_w(0)
                low_w(1)
                for u in range(LATE):
                    if UNITS[u][0] == "qk":
                        low_qk(0, UNITS[u][1], True)
                    if u == 1:
                        low_w(2)
                        low_w(3)
                        low_w(4)
                    if u in (1, 2):
                        maxes(0, 2 * u - 2)
                        maxes(0, 2 * u - 1)
                    if u == 3:
                        normalise(1, 0)
                    if u == 4:
                        scale(0, 0)
                    if u == 5:
                        scale(0, 1)
                    if u == 6:
                        normalise(1, 1)

                def step(n, t, before):
                    if t == 1 and before is not None:
                        dve.wait_ge(projected, before * PAIRS + PAIRS)
                        dve.wait_ge(bias_added, before + 1)
                        here = xs[:, bass.ds(2 * before, 2), :]
                        nc.vector.tensor_tensor(here, here, out_ps[:, 0:2 * D].rearrange("p (s d) -> p s d", d=D),
                                                ALU.add).then_inc(added, 1)
                    if t >= 1 and exists(n):
                        take_context(n, t - 1)
                    elif t == 0 and before is not None:
                        take_context(before, PAIRS - 1)
                    if t == 2 and exists(n + 1):
                        take_xn(n + 1)
                    for place in (EVEN, ODD):
                        m, h = later(n, 2 * t + place + SCALED_AHEAD)
                        if exists(m):
                            scale(m, h)
                        for unit_n, u in unit_at(n, t, place):
                            if UNITS[u][0] == "qk":
                                low_qk(unit_n, UNITS[u][1])
                        m, h = later(n, 2 * t + place + AHEAD)
                        if exists(m):
                            maxes(m, h)
                    if t in (3, 5) and exists(n + 2):
                        normalise(n + 2, (t - 3) // 2)
                all_steps(dve, step)

        with nc.Block() as block:
            feed_forward(block, 0, [(gate_proj, gate_raw, gate_hi, gate_lo), (up_proj, up_raw, up_hi, up_lo),
                                     (down_proj, down_raw, down_hi, down_lo)])
        with nc.Block() as block:
            attention(block)
        with nc.Block() as block:
            feed_forward(block, 1, [(down_proj, down_raw, down_hi, down_lo)])


_SHAPE = (16, 256, 128)


def kernel(**inputs):
    import numpy as _np
    import concourse.bacc as _bacc
    from concourse import mybir as _mybir
    from concourse.bass_utils import run_bass_kernel_spmd as _run

    a = {k[3:]: _np.asarray(v) for k, v in inputs.items()}
    def columns(w):
        w = w.reshape(GROUPS, GE, D, CPG, FS).transpose(2, 0, 3, 1, 4)
        return w.reshape(D, GROUPS, GW)
    down = a["ffn_down_proj"].reshape(GROUPS, GE, CPG, FS, D).transpose(1, 3, 0, 2, 4).reshape(P, GROUPS, GW)
    laid = {
        "x": a["attn_x"],
        "wq": a["attn_Wq"].T, "wk": a["attn_Wk"].T, "wv": a["attn_Wv"].T,
        "wo": a["attn_Wo"].T.reshape(PAIRS, P, D).transpose(1, 0, 2),
        "bo": a["attn_bo"].reshape(1, D),
        "gate_w": a["ffn_gate_w"].T,
        "gate_proj": columns(a["ffn_gate_proj"]), "up_proj": columns(a["ffn_up_proj"]), "down_proj": down,
    }
    nc = _bacc.Bacc("TRN2", target_bir_lowering=False, num_devices=1)
    arrays, args = {}, {}
    for name, v in laid.items():
        arrays[f"in_{name}"] = v = _np.ascontiguousarray(v)
        args[name] = nc.dram_tensor(f"in_{name}", v.shape, _mybir.dt.from_np(v.dtype), kind="ExternalInput").ap()
    args["out"] = nc.dram_tensor("out_x", _SHAPE, _mybir.dt.float32, kind="ExternalOutput").ap()
    macaron_block(nc, **args)
    r = _run(nc, [arrays], core_ids=[0])
    return r.results[0]["out_x"]
```
